# Optimizing a Trainium2 kernel written in Bass

```python
import numpy as np
import jax
import jax.numpy as jnp

def _softmax(x, axis=-1):
    return jax.nn.softmax(x, axis=axis)

def _gelu(x):
    return jax.nn.gelu(x, approximate=True)

def _silu(x):
    return jax.nn.silu(x)

def _sigmoid(x):
    return jax.nn.sigmoid(x)

def _layernorm(x, axis=-1, eps=1e-05):
    m = jnp.mean(x, axis=axis, keepdims=True)
    v = jnp.var(x, axis=axis, keepdims=True)
    return (x - m) / jnp.sqrt(v + eps)

def _scatter_add(tgt, idx, src, axis=0):
    return tgt.at[idx].add(src)

def _segment_sum(src, seg, n):
    return jax.ops.segment_sum(src, seg, n)
kernel_name = 'mk_seq_preln_d1_jaxref_r4_b33e4a'

def setup_inputs(seed: int=0):
    np.random.seed(seed)
    _w = jnp.asarray

    def _L0_attn_setup():
        import jax, jax.numpy as jnp
        import numpy as np
        EMB = 512
        HEADS = 16
        HEAD_DIM = EMB // HEADS
        SCALE = float(np.sqrt(HEAD_DIM))
        SRMS_SCALE = 1.0 / float(np.sqrt(HEAD_DIM))

        def _srms_norm(x, scale):
            xf = x.astype(jnp.float32)
            norm = jnp.linalg.norm(xf * scale, axis=-1, keepdims=True)
            norm = jnp.maximum(norm, 1e-12)
            return (xf / norm).astype(x.dtype)
        key = jax.random.key(seed)
        ks = jax.random.split(key, 6)
        B, L = (4, 1024)
        std = 1.0 / np.sqrt(EMB)
        return {'x': jax.random.normal(ks[0], (B, L, EMB), dtype=jnp.float32), 'wq': jax.random.normal(ks[1], (EMB, EMB), dtype=jnp.float32) * std, 'wk': jax.random.normal(ks[2], (EMB, EMB), dtype=jnp.float32) * std, 'wv': jax.random.normal(ks[3], (EMB, EMB), dtype=jnp.float32) * std, 'wu': jax.random.normal(ks[4], (EMB, EMB), dtype=jnp.float32) * std, 'wo': jax.random.normal(ks[5], (EMB, EMB), dtype=jnp.float32) * std}
    _L0_attn_in = _L0_attn_setup()

    def _L0_ffn_setup():
        import jax, jax.numpy as jnp
        import numpy as np
        TOP_K = 2

        def moe_forward(x, w_gate_router, w_gate_proj, w_up_proj, w_down_proj):
            E = w_gate_router.shape[0]
            scores = jnp.einsum('bsd,ed->bse', x, w_gate_router)
            topk_scores, topk_idx = jax.lax.top_k(scores, TOP_K)
            topk_probs = jax.nn.softmax(topk_scores, axis=-1)
            weights = jnp.sum(topk_probs[..., None] * jax.nn.one_hot(topk_idx, E, dtype=x.dtype), axis=-2)
            gate = jnp.einsum('bsd,efd->bsef', x, w_gate_proj)
            up = jnp.einsum('bsd,efd->bsef', x, w_up_proj)
            hidden = jax.nn.silu(gate) * up
            out = jnp.einsum('bsef,edf,bse->bsd', hidden, w_down_proj, weights)
            return out
        key = jax.random.key(seed)
        k1, k2, k3, k4, k5 = jax.random.split(key, 5)
        B, S, D, E, F = (2, 256, 512, 8, 192)
        scale_in = 1.0 / np.sqrt(D)
        scale_ff = 1.0 / np.sqrt(F)
        return {'x': jax.random.normal(k1, (B, S, D), dtype=jnp.float32), 'w_gate_router': jax.random.normal(k2, (E, D), dtype=jnp.float32) * scale_in, 'w_gate_proj': jax.random.normal(k3, (E, F, D), dtype=jnp.float32) * scale_in, 'w_up_proj': jax.random.normal(k4, (E, F, D), dtype=jnp.float32) * scale_in, 'w_down_proj': jax.random.normal(k5, (E, D, F), dtype=jnp.float32) * scale_ff}
    _L0_ffn_in = _L0_ffn_setup()
    _d = {'L0_attn_x': _L0_attn_in['x'], 'L0_attn_wq': _L0_attn_in['wq'], 'L0_attn_wk': _L0_attn_in['wk'], 'L0_attn_wv': _L0_attn_in['wv'], 'L0_attn_wu': _L0_attn_in['wu'], 'L0_attn_wo': _L0_attn_in['wo'], 'L0_ffn_w_gate_router': _L0_ffn_in['w_gate_router'], 'L0_ffn_w_gate_proj': _L0_ffn_in['w_gate_proj'], 'L0_ffn_w_up_proj': _L0_ffn_in['w_up_proj'], 'L0_ffn_w_down_proj': _L0_ffn_in['w_down_proj']}
    _x0 = _d['L0_attn_x']
    _d['L0_attn_x'] = jax.random.normal(jax.random.fold_in(jax.random.key(seed), 1), (2, 1024, 512), dtype=_x0.dtype)
    del _x0
    return _d

def reference(L0_attn_x, L0_attn_wq, L0_attn_wk, L0_attn_wv, L0_attn_wu, L0_attn_wo, L0_ffn_w_gate_router, L0_ffn_w_gate_proj, L0_ffn_w_up_proj, L0_ffn_w_down_proj):

    def _L0_attn_ref(x, wq, wk, wv, wu, wo):
        import jax, jax.numpy as jnp
        import numpy as np
        EMB = 512
        HEADS = 16
        HEAD_DIM = EMB // HEADS
        SCALE = float(np.sqrt(HEAD_DIM))
        SRMS_SCALE = 1.0 / float(np.sqrt(HEAD_DIM))

        def _srms_norm(x, scale):
            xf = x.astype(jnp.float32)
            norm = jnp.linalg.norm(xf * scale, axis=-1, keepdims=True)
            norm = jnp.maximum(norm, 1e-12)
            return (xf / norm).astype(x.dtype)
        B, L, D = x.shape
        H, hd = (HEADS, HEAD_DIM)

        def proj(w):
            t = jnp.einsum('bld,ed->ble', x, w)
            return t.reshape(B, L, H, hd).transpose(0, 2, 1, 3)
        Q = jax.nn.relu(proj(wq)) / SCALE
        K = jax.nn.relu(proj(wk)) / SCALE
        V = proj(wv)
        U = jax.nn.silu(proj(wu))
        KV = jnp.einsum('bhld,bhle->bhde', K, V)
        O = jnp.einsum('bhld,bhde->bhle', Q, KV)
        O = _srms_norm(O, SRMS_SCALE) * U
        O = O.transpose(0, 2, 1, 3).reshape(B, L, D)
        return jnp.einsum('bld,ed->ble', O, wo)

    def _L0_ffn_ref(x, w_gate_router, w_gate_proj, w_up_proj, w_down_proj):
        import jax, jax.numpy as jnp
        import numpy as np
        TOP_K = 2

        def moe_forward(x, w_gate_router, w_gate_proj, w_up_proj, w_down_proj):
            E = w_gate_router.shape[0]
            scores = jnp.einsum('bsd,ed->bse', x, w_gate_router)
            topk_scores, topk_idx = jax.lax.top_k(scores, TOP_K)
            topk_probs = jax.nn.softmax(topk_scores, axis=-1)
            weights = jnp.sum(topk_probs[..., None] * jax.nn.one_hot(topk_idx, E, dtype=x.dtype), axis=-2)
            gate = jnp.einsum('bsd,efd->bsef', x, w_gate_proj)
            up = jnp.einsum('bsd,efd->bsef', x, w_up_proj)
            hidden = jax.nn.silu(gate) * up
            out = jnp.einsum('bsef,edf,bse->bsd', hidden, w_down_proj, weights)
            return out
        return moe_forward(x, w_gate_router, w_gate_proj, w_up_proj, w_down_proj)
    x = L0_attn_x
    x = x + _L0_attn_ref(_layernorm(x, axis=-1), L0_attn_wq, L0_attn_wk, L0_attn_wv, L0_attn_wu, L0_attn_wo)
    x = x + _L0_ffn_ref(_layernorm(x, axis=-1), L0_ffn_w_gate_router, L0_ffn_w_gate_proj, L0_ffn_w_up_proj, L0_ffn_w_down_proj)
    return x

_drawn_inputs = setup_inputs


def setup_inputs(seed=0):
    import zlib

    import numpy as np

    out = dict(_drawn_inputs(seed))
    spreads = {}
    factors = {}
    for name, (base, spread) in spreads.items():
        noise = np.random.default_rng([zlib.crc32(name.encode()), seed]).standard_normal(out[name].shape)
        drawn = base * np.exp(spread * noise) if base else spread * noise
        out[name] = jnp.asarray(drawn.astype(out[name].dtype))
    for name, factor in factors.items():
        out[name] = (out[name] * factor).astype(out[name].dtype)
    return out
```

```python
from contextlib import ExitStack

import concourse.bass as bass
from concourse import mybir

ALU = mybir.AluOpType
ACT = mybir.ActivationFunctionType
F32 = mybir.dt.float32
BF16 = mybir.dt.bfloat16
I32 = mybir.dt.int32
U32 = mybir.dt.uint32
AX_X = mybir.AxisListType.X

P = 128
D = 512
C = D // P
HD = 32
H = D // HD
G = P // HD
E = 8
F = 192
FP = 96
FH = F // FP
EPS = 1e-5


def attention_and_moe(nc, x, wqkvu, wo, wrouter, wgateup, wdown, h_dram, y_dram, out):
    T = x.shape[0]
    B = 2
    L = T // B
    NT = T // P
    TB = L // P
    BLK = 4
    NB = TB // BLK
    NPAIR = 2 * T
    NS = (NPAIR + E * (P - 1)) // P
    R2 = 2 * NT

    with ExitStack() as ctx:
        def sb(name, shape, dt=F32):
            return ctx.enter_context(nc.sbuf_tensor(name, shape, dt))

        def sem(name):
            return ctx.enter_context(nc.semaphore(name))

        w_attn = sb("w_attn", [P, 4, C, D])
        w_o = sb("w_o", [P, C, D])
        w_r = sb("w_r", [P, C, E])
        w_gu = sb("w_gu", [P, E, C * 2 * F])
        w_dn = w_attn[0:FP, :, :, :].rearrange("p a c n -> p (a c n)").rearrange("p (e n) -> p e n", e=E)
        rows = sb("rows", [P, NT, D])
        ident = sb("ident", [P, P])
        expo = sb("expo", [P, H])

        arena_size = 2 * C * BLK * P + C * L + TB * D + 4 * D + C * P + 2 * D + 4 * D + 4 * C * P
        arena = sb("arena", [P, arena_size])
        used = [0]

        def carve(n):
            used[0] += n
            assert used[0] <= arena_size, (used[0], arena_size)
            return arena[:, used[0] - n:used[0]]

        xT = carve(NB * C * BLK * P).rearrange("p (b c n) -> p b c n", b=NB, c=C)
        qT = carve(C * L).rearrange("p (c n) -> p c n", c=C)
        u = carve(TB * D).rearrange("p (t n) -> p t n", t=TB)
        k_sb = carve(2 * D).rearrange("p (b n) -> p b n", b=2)
        v_sb = carve(2 * D).rearrange("p (b n) -> p b n", b=2)
        kv_bd = carve(C * P).rearrange("p (c n) -> p c n", c=C)
        xn = carve(2 * D).rearrange("p (b n) -> p b n", b=2)
        sq = k_sb
        att = carve(2 * D).rearrange("p (b n) -> p b n", b=2)
        h_sb = carve(2 * D).rearrange("p (b n) -> p b n", b=2)
        attT = carve(2 * C * P).rearrange("p (b c n) -> p b c n", b=2, c=C)
        hT = carve(2 * C * P).rearrange("p (b c n) -> p b c n", b=2, c=C)
        used[0] = 0
        xg = carve(2 * D).rearrange("p (b n) -> p b n", b=2)
        xgT = carve(2 * C * P).rearrange("p (b c n) -> p b c n", b=2, c=C)
        sg = carve(2 * F).rearrange("p (b n) -> p b n", b=2)
        hid = carve(2 * F).rearrange("p (b n) -> p b n", b=2)
        hidT = carve(2 * FH * P).rearrange("p (b c n) -> p b c n", b=2, c=FH)
        y_sb = carve(2 * D).rearrange("p (b n) -> p b n", b=2)
        ya = carve(4 * D).rearrange("p (b n) -> p b n", b=4)
        yb = carve(4 * D).rearrange("p (b n) -> p b n", b=4)
        hot = [carve(NT * E).rearrange("p (t e) -> p t e", t=NT) for _ in range(2)]
        slot_all = carve(NT * E).rearrange("p (t e) -> p t e", t=NT)
        picked = carve(NT * E).rearrange("p (t e) -> p t e", t=NT)
        above = carve(E * NT).rearrange("p (e k) -> p e k", e=E)
        before = carve(NS * E).rearrange("p (s e) -> p s e", s=NS)
        iota_hi = carve(R2 * NS).rearrange("p (r s) -> p r s", r=R2)
        iota_lo = carve(P)
        hit_lo = carve(R2 * P // 2).bitcast(BF16).rearrange("p (r n) -> p r n", r=R2)
        hit_hi = carve(R2 * NS).rearrange("p (r s) -> p r s", r=R2)
        id_hi = carve(R2 * NS).bitcast(BF16).rearrange("p (r a s) -> p r a s", r=R2, a=2)

        bstat = sb("bstat", [P, BLK, 6])
        mv = sb("mv", [P, BLK, 2])
        rstd = sb("rstd", [P, 2, BLK])
        ss = sb("ss", [P, 2, H])
        rn = sb("rn", [P, 2, H])
        rn_in = sb("rn_in", [P, H])
        scores = sb("scores", [P, NT, E])
        top = sb("top", [P, NT, E])
        top_id = sb("top_id", [P, NT, E], U32)
        top_idf = sb("top_idf", [P, 2, NT])
        mask = sb("mask", [P, NT, E], BF16)
        iota_e = sb("iota_e", [P, E])
        thresh = sb("thresh", [P, NT])
        upto = sb("upto", [P, E, E])
        js = sb("js", [P, NS])
        nums = sb("nums", [P, 4, E])
        slotf = sb("slotf", [P, 2, NT])
        slot = sb("slot", [P, 2, NT], I32)
        lo_i = sb("lo_i", [P, 2, NT], I32)
        hi_i = sb("hi_i", [P, 2, NT], I32)
        lo_f = sb("lo_f", [P, 2 * NT])
        hi_f = sb("hi_f", [P, 2 * NT])
        part = sb("part", [P, 1])
        tile_no = sb("tile_no", [P, NT])
        tri = sb("tri", [P, P], BF16)
        ones = sb("ones", [P, P], BF16)
        token_f = sb("token_f", [P, 2, NS])
        token = sb("token", [P, NS], U32)
        expert_f = sb("expert_f", [P, NS])
        expert = sb("expert", [P, NS], I32)
        pick = sb("pick", [P, 2], U32)
        gap = sb("gap", [P, NT])
        egap = sb("egap", [P, NT])
        prob = sb("prob", [P, 2, NT])

        ps = [ctx.enter_context(nc.psum_tensor(f"ps{i}", [P, 512], F32)) for i in range(8)]
        tp = ps[0:2]
        pj = ps[2:5]
        kv_ps = ps[5]
        o_ps = ps[6:8]

        s_x = [sem(f"x_loaded{i}") for i in range(NB)]
        s_w = [sem(f"w_loaded_{n}") for n in "qkvuo"]
        s_wr = sem("router_loaded")
        s_wgu = sem("gateup_loaded")
        s_wdn = sem("down_loaded")
        s_const = sem("constants_made")
        s_bst = sem("stats_made")
        s_var = sem("var_made")
        s_rsi = sem("rstd_base_made")
        s_rstd = sem("rstd_made")
        s_xn = sem("xn_made")
        s_h = sem("h_made")
        s_hsaved = [sem(f"h_saved{i}") for i in range(2)]
        s_tp = sem("transposed")
        s_tpst = sem("transposed_stored")
        s_kvf = sem("k_or_v_filled")
        s_kvs = sem("k_or_v_stored")
        s_uf, s_us = sem("u_filled"), sem("u_stored")
        s_qf, s_qs = sem("q_filled"), sem("q_stored")
        s_kvused = sem("kv_used")
        s_sts = sem("state_stored")
        s_of = sem("o_filled")
        s_sq = sem("squares_made")
        s_ss = sem("square_sums_made")
        s_rni = sem("norm_base_made")
        s_rn = sem("norm_made")
        s_a1 = sem("normed")
        s_att = sem("gated")
        s_pf, s_x1 = sem("attn_out_filled"), sem("x1_made")
        s_rf, s_sc = sem("scores_filled"), sem("scores_stored")
        GAP_MADE, MASK_MADE, IDS_MADE = 3, 7, 24
        s_v = sem("routing_step_vector")
        s_cnt = sem("ranks_filled")
        s_eg = sem("exp_made")
        s_tok = sem("tokens_filled")
        s_route = sem("routing_made")
        s_pick = sem("pick_made")
        s_xg = [sem(f"gathered{i}") for i in range(2)]
        s_xgt, s_xgs = sem("slots_transposed"), sem("slots_stored")
        s_guf, s_sg, s_hid = sem("gateup_filled"), sem("silu_made"), sem("hidden_made")
        s_ht, s_hts = sem("hidden_transposed"), sem("hidden_stored")
        s_yf, s_ys = sem("y_filled"), sem("y_stored")
        s_ysv = [sem(f"y_saved{i}") for i in range(2)]
        s_cpick = sem("combine_pick_made")
        s_ya = [sem(f"y_gathered{i}") for i in range(4)]
        s_c1, s_c2 = sem("first_choice_added"), sem("second_choice_added")
        s_out = [sem(f"out_saved{i}") for i in range(4)]

        STEPS_B = TB + 5
        tp_order, pj_order = [], []
        tp_order += [("x", t) for t in range(BLK)]
        for i in range(TB):
            pj_order += [("k", i), ("v", i), ("u", i)]
            if i + BLK < TB:
                tp_order.append(("x", i + BLK))
            if i % BLK == BLK - 1:
                pj_order += [("q", (i // BLK) * C + c) for c in range(C)]
        for s in range(STEPS_B):
            if 2 <= s < TB + 2:
                tp_order.append(("a", s - 2))
                pj_order.append(("p", s - 2))
            if 4 <= s < TB + 4:
                tp_order.append(("h", s - 4))
            if 5 <= s < TB + 5:
                pj_order.append(("r", s - 5))
        NTP, NPJ = len(tp_order), len(pj_order)
        assert NTP % 2 == 0 and NPJ % 3 == 0
        tp_at = {key: n for n, key in enumerate(tp_order)}
        pj_at = {key: n for n, key in enumerate(pj_order)}
        PJ_STORE = {"k": (s_kvs, 2 * TB, lambda i: 2 * i + 1), "v": (s_kvs, 2 * TB, lambda i: 2 * i + 2),
                    "u": (s_us, TB, lambda i: i + 1), "q": (s_qs, NB * C, lambda i: i + 1),
                    "p": (s_x1, TB, lambda i: i + 1), "r": (s_sc, TB, lambda i: i + 1)}

        def pj_bank(key):
            return pj[pj_at[key] % 3]

        def tp_bank(key):
            return tp[tp_at[key] % 2]

        block = ctx.enter_context(nc.Block())

        @block.sync
        def _(sp):
            xb = x.rearrange("(g t p) n -> g p t n", p=P, t=BLK)
            sp.dma_start(rows[:, 0:BLK, :], xb[0]).then_inc(s_x[0], 16)
            sp.dma_start(w_attn[:, 1], wqkvu[1]).then_inc(s_w[1], 16)
            sp.dma_start(w_attn[:, 2], wqkvu[2]).then_inc(s_w[2], 16)
            sp.dma_start(w_attn[:, 3], wqkvu[3]).then_inc(s_w[3], 16)
            sp.dma_start(rows[:, BLK:2 * BLK, :], xb[1]).then_inc(s_x[1], 16)
            sp.dma_start(w_attn[:, 0], wqkvu[0]).then_inc(s_w[0], 16)
            sp.dma_start(w_o[:], wo).then_inc(s_w[4], 16)
            sp.dma_start(w_r[:], wrouter).then_inc(s_wr, 16)
            for k in range(NB):
                sp.wait_ge(s_x[k], 16)
                sp.dma_start(rows[:, (NB + k) * BLK:(NB + k + 1) * BLK, :], xb[NB + k]).then_inc(s_x[k], 16)
            sp.dma_start(w_gu[:], wgateup).then_inc(s_wgu, 16)
            with sp.Fori(0, NT // 2) as i:
                for k in range(2):
                    sp.wait_ge(s_h, 2 * i + k + 1)
                    sp.dma_start(h_dram[bass.ds((2 * i + k) * P, P), :], h_sb[:, k, :]).then_inc(s_hsaved[k], 16)
            sp.wait_ge(s_qf, B * NB * C)
            sp.wait_ge(s_uf, B * TB)
            sp.dma_start(w_dn, wdown).then_inc(s_wdn, 16)
            with sp.Fori(0, NS // 2) as i:
                for k in range(2):
                    sp.wait_ge(s_ys, 2 * i + k + 1)
                    sp.dma_start(y_dram[bass.ds((2 * i + k) * P, P), :], y_sb[:, k, :]).then_inc(s_ysv[k], 16)
            sp.wait_ge(s_ys, NS)
            sp.dma_start(y_dram[(NS - 1) * P:NS * P, :], y_sb[:, 0, :]).then_inc(s_ysv[0], 16)
            with sp.Fori(0, NT // 4) as i:
                for k in range(4):
                    sp.wait_ge(s_c2, 4 * i + k + 1)
                    sp.dma_start(out[bass.ds((4 * i + k) * P, P), :], ya[:, k, :]).then_inc(s_out[k], 16)
            for k in range(4):
                sp.wait_ge(s_out[k], 16 * (NT // 4))

        @block.gpsimd
        def _(pool):
            def made(ins):
                ins.then_inc(s_const, 1)

            made(nc.gpsimd.memset(ident[:], 0.0))
            made(nc.gpsimd.memset(expo[:], -0.5))
            made(nc.gpsimd.memset(tri[:], 0.0))
            made(nc.gpsimd.memset(ones[:], 1.0))
            pool.wait_ge(s_const, 4)
            made(nc.gpsimd.affine_select(out=ident[:], in_=ident[:], compare_op=ALU.not_equal, fill=1.0,
                                         base=0, pattern=[[-1, P]], channel_multiplier=1))
            made(nc.gpsimd.affine_select(out=tri[:], in_=tri[:], compare_op=ALU.is_ge, fill=1.0,
                                         base=0, pattern=[[-1, P]], channel_multiplier=1))
            made(nc.gpsimd.iota(part[:], pattern=[[0, 1]], base=0, channel_multiplier=1,
                                allow_small_or_imprecise_dtypes=True))
            made(nc.gpsimd.iota(tile_no[:], pattern=[[1, NT]], base=0, channel_multiplier=0,
                                allow_small_or_imprecise_dtypes=True))
            made(nc.gpsimd.iota(iota_e[:], pattern=[[1, E]], base=0, channel_multiplier=0,
                                allow_small_or_imprecise_dtypes=True))
            made(nc.gpsimd.iota(thresh[:], pattern=[[P, NT]], base=0, channel_multiplier=0,
                                allow_small_or_imprecise_dtypes=True))
            made(nc.gpsimd.iota(js[:], pattern=[[1, NS]], base=0, channel_multiplier=0,
                                allow_small_or_imprecise_dtypes=True))
            made(nc.gpsimd.memset(upto[:], 1.0))
            pool.wait_ge(s_const, 12)
            made(nc.gpsimd.affine_select(out=upto[:], in_=upto[:], compare_op=ALU.is_ge, fill=0.0,
                                         base=0, pattern=[[1, E], [-1, E]], channel_multiplier=0))

            def inverse_root(out_ap, in_ap, n, steps, done):
                nc.gpsimd.tensor_tensor(out_ap, in_ap, expo[:, 0:n], ALU.pow).then_inc(done, 1)

            with pool.Fori(0, B) as b:
                for g in range(NB):
                    pool.wait_ge(s_rsi, b * (NB + TB) + g + 1)
                    inverse_root(rstd[:, g % 2, :], rstd[:, g % 2, :], BLK, None, s_rstd)
                for s in range(STEPS_B):
                    if s < TB:
                        pool.wait_ge(s_ss, b * TB + s + 1)
                        pool.nop(nofuse=True)
                        nc.gpsimd.tensor_scalar(rn_in[:], ss[:, s % 2, :], 1e-24, 1024.0, ALU.max, ALU.mult)\
                            .then_inc(s_rni, 1)
                        pool.wait_ge(s_rni, b * TB + s + 1)
                        inverse_root(rn[:, s % 2, :], rn_in[:], H, None, s_rn)
                    if 2 <= s < TB + 2:
                        j = s - 2
                        pool.wait_ge(s_rsi, b * (NB + TB) + NB + j + 1)
                        inverse_root(rstd[:, j % 2, 0:1], rstd[:, j % 2, 0:1], 1, None, s_rstd)

            pool.wait_ge(s_v, 1)
            nc.gpsimd.iota(iota_hi[:], pattern=[[0, R2], [1, NS]], base=0, channel_multiplier=0,
                           allow_small_or_imprecise_dtypes=True).then_inc(s_const, 1)
            nc.gpsimd.iota(iota_lo[:], pattern=[[1, P]], base=0, channel_multiplier=0,
                           allow_small_or_imprecise_dtypes=True).then_inc(s_const, 1)

            def gather(j, k, first):
                if not first:
                    pool.wait_ge(s_xg[k], 16 * ((j - k) // 2))
                    pool.wait_ge(s_xgt, j - 1)
                nc.gpsimd.tensor_copy(pick[:, k:k + 1], token[:, bass.ds(j, 1)]).then_inc(s_pick, 1)
                pool.wait_ge(s_pick, j + 1)
                nc.gpsimd.indirect_dma_start(
                    out=xg[:, k, :], out_offset=None, in_=h_dram,
                    in_offset=bass.IndirectOffsetOnAxis(ap=pick[:, k:k + 1], axis=0)).then_inc(s_xg[k], 16)

            pool.wait_ge(s_route, 1)
            for k in range(2):
                pool.wait_ge(s_hsaved[k], 16 * (NT // 2))
            for j in range(2):
                gather(j, j, True)
            with pool.Fori(1, NS // 2) as i:
                for k in range(2):
                    jj = pool.snap(2 * i + k)
                    pool.wait_ge(s_xg[k], 16 * i)
                    pool.wait_ge(s_xgt, 2 * i + k - 1)
                    nc.gpsimd.tensor_copy(pick[:, k:k + 1], token[:, bass.ds(jj, 1)]).then_inc(s_pick, 1)
                    pool.wait_ge(s_pick, jj + 1)
                    pool.nop(nofuse=True)
                    nc.gpsimd.indirect_dma_start(
                        out=xg[:, k, :], out_offset=None, in_=h_dram,
                        in_offset=bass.IndirectOffsetOnAxis(ap=pick[:, k:k + 1], axis=0)).then_inc(s_xg[k], 16)
            gather(NS - 1, 0, False)

            pool.wait_ge(s_ysv[0], 16 * ((NS + 1) // 2))
            pool.wait_ge(s_ysv[1], 16 * (NS // 2))
            for t in range(NT):
                k = t % 4
                if t >= 4:
                    pool.wait_ge(s_out[k], 16 * (t // 4))
                for r, dst in ((0, ya), (1, yb)):
                    nc.gpsimd.indirect_dma_start(
                        out=dst[:, k, :], out_offset=None, in_=y_dram,
                        in_offset=bass.IndirectOffsetOnAxis(ap=slot[:, r, t:t + 1].bitcast(U32), axis=0))\
                        .then_inc(s_ya[k], 16)

        @block.scalar
        def _(act):
            def store_tp(b, key, dst):
                n = tp_at[key]
                act.wait_ge(s_tp, b * NTP + n + 1)
                nc.scalar.activation(dst, tp_bank(key)[:].rearrange("p (c n) -> p c n", c=C), ACT.Copy)\
                    .then_inc(s_tpst, 1)

            with act.Fori(0, B) as b:
                for t in range(BLK):
                    store_tp(b, ("x", t), xT[:, 0, :, t * P:(t + 1) * P])
                for i in range(TB):
                    act.wait_ge(s_uf, b * TB + i + 1)
                    nc.scalar.activation(u[:, i, :], pj_bank(("u", i))[:], ACT.Silu).then_inc(s_us, 1)
                    if i + BLK < TB:
                        n = i + BLK
                        store_tp(b, ("x", n), xT[:, n // BLK, :, (n % BLK) * P:(n % BLK + 1) * P])
                    if i % BLK == BLK - 1:
                        g = i // BLK
                        for c in range(C):
                            act.wait_ge(s_qf, b * NB * C + g * C + c + 1)
                            nc.scalar.activation(qT[:, c, g * BLK * P:(g + 1) * BLK * P],
                                                 pj_bank(("q", g * C + c))[:], ACT.Relu).then_inc(s_qs, 1)
                for s in range(STEPS_B):
                    if s < TB:
                        act.wait_ge(s_of, b * TB + s + 1)
                        if s >= 2:
                            act.wait_ge(s_ss, b * TB + s - 1)
                        nc.scalar.activation(sq[:, s % 2, :], o_ps[s % 2][:], ACT.Square,
                                             scale=1.0 / (HD * HD ** 0.5)).then_inc(s_sq, 1)
                    if 2 <= s < TB + 2:
                        j = s - 2
                        if j >= 2:
                            act.wait_ge(s_pf, b * TB + j - 1)
                        store_tp(b, ("a", j), attT[:, j % 2])
                    if 4 <= s < TB + 4:
                        j = s - 4
                        if j >= 2:
                            act.wait_ge(s_rf, b * TB + j - 1)
                        store_tp(b, ("h", j), hT[:, j % 2])
                act.wait_ge(s_ss, (b + 1) * TB)
                act.wait_ge(s_pf, (b + 1) * TB)
                act.wait_ge(s_rf, (b + 1) * TB)
            act.wait_ge(s_v, GAP_MADE)
            nc.scalar.activation(egap[:], gap[:], ACT.Exp).then_inc(s_eg, 1)

            def store_x(j, k):
                act.wait_ge(s_xgt, j + 1)
                nc.scalar.activation(xgT[:, k], ps[k][:].rearrange("p (c n) -> p c n", c=C), ACT.Copy)\
                    .then_inc(s_xgs, 1)

            def silu(j, k, first):
                act.wait_ge(s_guf, j + 1)
                if not first:
                    act.wait_ge(s_hid, j - 1)
                nc.scalar.activation(sg[:, k, :], ps[2 + k][:, 0:F], ACT.Silu).then_inc(s_sg, 1)

            store_x(0, 0)
            silu(0, 0, True)
            store_x(1, 1)
            silu(1, 1, True)
            store_x(2, 0)
            with act.Fori(1, NS // 2) as i:
                silu(2 * i, 0, False)
                store_x(2 * i + 1, 1)
                silu(2 * i + 1, 1, False)
                store_x(2 * i + 2, 0)
            silu(NS - 1, 0, False)

        @block.vector
        def _(dve):
            def normalise(b, i):
                g, t = i // BLK, i % BLK
                if i >= 2:
                    dve.wait_ge(s_tp, b * NTP + tp_at[("x", i - 2)] + 1)
                nc.vector.tensor_scalar(xn[:, i % 2, :], rows[:, bass.ds(b * TB + i, 1), :]
                                        .rearrange("p a n -> p (a n)"), mv[:, t, 0:1],
                                        rstd[:, g % 2, t:t + 1], ALU.subtract, ALU.mult).then_inc(s_xn, 1)

            with dve.Fori(0, B) as b:
                for g in range(NB):
                    dve.wait_ge(s_x[g], 16 * b + 16)
                    dve.nop(nofuse=True)
                    for t in range(BLK):
                        nc.vector.bn_stats(bstat[:, t, :], rows[:, bass.ds(b * TB + g * BLK + t, 1), :]
                                           .rearrange("p a n -> p (a n)")).then_inc(s_bst, 1)
                    dve.wait_ge(s_bst, b * 2 * TB + (g + 1) * BLK)
                    dve.nop(nofuse=True)
                    for t in range(BLK):
                        nc.vector.bn_aggr(mv[:, t, :], bstat[:, t, :]).then_inc(s_var, 1)
                    dve.wait_ge(s_var, b * 2 * TB + (g + 1) * BLK)
                    nc.vector.tensor_scalar(rstd[:, g % 2, :], mv[:, :, 1], EPS, None, ALU.add).then_inc(s_rsi, 1)
                    dve.wait_ge(s_rstd, b * (NB + TB) + g + 1)
                    for i in range(g * BLK, min((g + 1) * BLK, BLK + 2)):
                        normalise(b, i)
                for i in range(TB):
                    if i >= 2:
                        dve.wait_ge(s_kvused, b * TB + i - 1)
                    dve.wait_ge(s_kvf, b * 2 * TB + 2 * i + 1)
                    nc.vector.tensor_scalar(k_sb[:, i % 2, :], pj_bank(("k", i))[:], 0.0, None, ALU.max)\
                        .then_inc(s_kvs, 1)
                    dve.wait_ge(s_kvf, b * 2 * TB + 2 * i + 2)
                    nc.vector.tensor_copy(v_sb[:, i % 2, :], pj_bank(("v", i))[:]).then_inc(s_kvs, 1)
                    if i + BLK + 2 < TB:
                        normalise(b, i + BLK + 2)
                nc.vector.memset(kv_bd[:], 0.0).then_inc(s_sts, 1)
                dve.wait_ge(s_sts, b * (1 + G) + 1)
                dve.wait_ge(s_kvused, b * TB + TB)
                for q in range(G):
                    src = kv_ps[q * HD:(q + 1) * HD, :].rearrange("p (c n) -> p c n", c=C)
                    nc.vector.tensor_copy(kv_bd[q * HD:(q + 1) * HD, :, q * HD:(q + 1) * HD],
                                          src[:, :, q * HD:(q + 1) * HD]).then_inc(s_sts, 1)
                for s in range(STEPS_B):
                    if s < TB:
                        dve.wait_ge(s_sq, b * TB + s + 1)
                        nc.vector.tensor_reduce(ss[:, s % 2, :], sq[:, s % 2, :].rearrange("p (h e) -> p h e", e=HD),
                                                axis=AX_X, op=ALU.add).then_inc(s_ss, 1)
                        dve.wait_ge(s_rn, b * TB + s + 1)
                        if s >= 2:
                            dve.wait_ge(s_tp, b * NTP + tp_at[("a", s - 2)] + 1)
                        nc.vector.tensor_tensor(
                            att[:, s % 2, :].rearrange("p (h e) -> p h e", e=HD),
                            o_ps[s % 2][:].rearrange("p (h e) -> p h e", e=HD),
                            rn[:, s % 2, :].unsqueeze(2).to_broadcast([P, H, HD]), ALU.mult).then_inc(s_a1, 1)
                        dve.wait_ge(s_a1, b * TB + s + 1)
                        dve.wait_ge(s_us, b * TB + s + 1)
                        nc.vector.tensor_tensor(att[:, s % 2, :], att[:, s % 2, :], u[:, s, :], ALU.mult)\
                            .then_inc(s_att, 1)
                    if 2 <= s < TB + 2:
                        j = s - 2
                        row = rows[:, bass.ds(b * TB + j, 1), :].rearrange("p a n -> p (a n)")
                        dve.wait_ge(s_pf, b * TB + j + 1)
                        nc.vector.tensor_tensor(row, pj_bank(("p", j))[:], row, ALU.add).then_inc(s_x1, 1)
                        dve.wait_ge(s_x1, b * TB + j + 1)
                        dve.nop(nofuse=True)
                        nc.vector.bn_stats(bstat[:, 0, :], row).then_inc(s_bst, 1)
                        dve.wait_ge(s_bst, b * 2 * TB + TB + j + 1)
                        dve.nop(nofuse=True)
                        nc.vector.bn_aggr(mv[:, 0, :], bstat[:, 0, :]).then_inc(s_var, 1)
                        dve.wait_ge(s_var, b * 2 * TB + TB + j + 1)
                        nc.vector.tensor_scalar(rstd[:, j % 2, 0:1], mv[:, 0, 1:2], EPS, None, ALU.add)\
                            .then_inc(s_rsi, 1)
                        dve.wait_ge(s_rstd, b * (NB + TB) + NB + j + 1)
                        if j >= 2:
                            dve.wait_ge(s_tp, b * NTP + tp_at[("h", j - 2)] + 1)
                            dve.wait_ge(s_hsaved[j % 2], 16 * (b * (TB // 2) + j // 2))
                        nc.vector.tensor_scalar(h_sb[:, j % 2, :], row, mv[:, 0, 0:1], rstd[:, j % 2, 0:1],
                                                ALU.subtract, ALU.mult).then_inc(s_h, 1)
                    if 5 <= s < TB + 5:
                        j = s - 5
                        dve.wait_ge(s_rf, b * TB + j + 1)
                        nc.vector.tensor_copy(scores[:, bass.ds(b * TB + j, 1), :].rearrange("p a e -> p (a e)"),
                                              pj_bank(("r", j))[:, 0:E]).then_inc(s_sc, 1)
                dve.wait_ge(s_tp, (b + 1) * NTP)
                for k in range(2):
                    dve.wait_ge(s_hsaved[k], 16 * (TB // 2) * (b + 1))

            steps = [0]

            def step(ins):
                steps[0] += 1
                ins.then_inc(s_v, 1)
                dve.wait_ge(s_v, steps[0])

            dve.wait_ge(s_sc, B * TB)
            step(nc.vector.tensor_copy(top[:, :, :], scores[:, :, :]))
            for t in range(NT):
                last = nc.vector.max(top[:, t, :], scores[:, t, :])
            step(last)
            step(nc.vector.tensor_tensor(gap[:], top[:, :, 1], top[:, :, 0], ALU.subtract))
            assert steps[0] == GAP_MADE
            for t in range(NT):
                last = nc.vector.max_index(top_id[:, t, :], top[:, t, :], scores[:, t, :])
            step(last)
            step(nc.vector.tensor_copy(top_idf[:], top_id[:, :, 0:2].rearrange("p t r -> p r t")))
            for r in range(2):
                last = nc.vector.tensor_tensor(hot[r], iota_e[:].unsqueeze(1).to_broadcast([P, NT, E]),
                                               top_idf[:, r, :].unsqueeze(2).to_broadcast([P, NT, E]), ALU.is_equal)
            step(last)
            step(nc.vector.tensor_tensor(mask[:], hot[0], hot[1], ALU.add))
            assert steps[0] == MASK_MADE
            dve.wait_ge(s_cnt, 1)
            step(nc.vector.tensor_copy(nums[:, 0, :], ps[1][:, 0:E]))
            step(nc.vector.tensor_tensor(above, nums[:, 0, :].unsqueeze(2).to_broadcast([P, E, NT]),
                                         thresh[:].unsqueeze(1).to_broadcast([P, E, NT]), ALU.is_gt))
            step(nc.vector.tensor_reduce(nums[:, 1, :], above, axis=AX_X, op=ALU.add))
            step(nc.vector.tensor_tensor(before[:, 0:E, :], nums[:, 1, :].unsqueeze(1).to_broadcast([P, E, E]),
                                         upto[:], ALU.mult))
            step(nc.vector.tensor_reduce(nums[:, 2, :], before[:, 0:E, :], axis=AX_X, op=ALU.add))
            step(nc.vector.tensor_tensor(nums[:, 3, :], nums[:, 2, :], nums[:, 1, :], ALU.subtract))
            step(nc.vector.tensor_scalar(nums[:, 3, :], nums[:, 3, :], float(P), None, ALU.mult))
            step(nc.vector.tensor_tensor(slot_all, ps[0][:, 0:NT * E].rearrange("p (t e) -> p t e", t=NT),
                                         nums[:, 3, :].unsqueeze(1).to_broadcast([P, NT, E]), ALU.add))
            for r in range(2):
                step(nc.vector.tensor_tensor(picked, slot_all, hot[r], ALU.mult))
                step(nc.vector.tensor_reduce(slotf[:, r, :], picked, axis=AX_X, op=ALU.add))
            step(nc.vector.tensor_copy(slot[:], slotf[:]))
            nc.vector.tensor_scalar(lo_i[:], slot[:], P - 1, None, ALU.bitwise_and)
            step(nc.vector.tensor_scalar(hi_i[:], slot[:], P.bit_length() - 1, None, ALU.logical_shift_right))
            nc.vector.tensor_copy(lo_f[:], lo_i[:].rearrange("p r t -> p (r t)"))
            step(nc.vector.tensor_copy(hi_f[:], hi_i[:].rearrange("p r t -> p (r t)")))
            dve.wait_ge(s_const, 15)
            nc.vector.tensor_tensor(hit_lo, iota_lo.unsqueeze(1).to_broadcast([P, R2, P]),
                                    lo_f[:].unsqueeze(2).to_broadcast([P, R2, P]), ALU.is_equal)
            step(nc.vector.tensor_tensor(hit_hi, iota_hi, hi_f[:].unsqueeze(2).to_broadcast([P, R2, NS]),
                                         ALU.is_equal))
            nc.vector.tensor_scalar(id_hi[:, :, 0, :], hit_hi, part[:], None, ALU.mult)
            for r in range(2):
                last = nc.vector.tensor_tensor(id_hi[:, r * NT:(r + 1) * NT, 1, :], hit_hi[:, r * NT:(r + 1) * NT, :],
                                               tile_no[:].unsqueeze(2).to_broadcast([P, NT, NS]), ALU.mult)
            step(last)
            assert steps[0] == IDS_MADE
            step(nc.vector.tensor_tensor(before, nums[:, 2, :].unsqueeze(1).to_broadcast([P, NS, E]),
                                         js[:].unsqueeze(2).to_broadcast([P, NS, E]), ALU.is_le))
            step(nc.vector.tensor_reduce(expert_f[:], before, axis=AX_X, op=ALU.add))
            step(nc.vector.tensor_scalar(expert[:], expert_f[:], float(E - 1), None, ALU.min))
            dve.wait_ge(s_eg, 1)
            step(nc.vector.tensor_scalar(gap[:], egap[:], 1.0, None, ALU.add))
            step(nc.vector.reciprocal(prob[:, 0, :], gap[:]))
            step(nc.vector.tensor_tensor(prob[:, 1, :], prob[:, 0, :], egap[:], ALU.mult))
            dve.wait_ge(s_tok, 1)
            step(nc.vector.tensor_copy(token_f[:], ps[2][:, 0:2 * NS].rearrange("p (a s) -> p a s", a=2)))
            nc.vector.scalar_tensor_tensor(out=token[:], in0=token_f[:, 1, :], scalar=float(P), in1=token_f[:, 0, :],
                                           op0=ALU.mult, op1=ALU.add).then_inc(s_route, 1)

            def hidden(j, k, first):
                dve.wait_ge(s_sg, j + 1)
                if not first:
                    dve.wait_ge(s_ht, j - 1)
                nc.vector.tensor_tensor(hid[:, k, :], ps[2 + k][:, F:2 * F], sg[:, k, :], ALU.mult)\
                    .then_inc(s_hid, 1)

            def store_hidden(j, k, first):
                dve.wait_ge(s_ht, j + 1)
                if not first:
                    dve.wait_ge(s_yf, j - 1)
                nc.vector.tensor_copy(hidT[0:FP, k], ps[4 + k][0:FP, 0:FH * P].rearrange("p (c n) -> p c n", c=FH))\
                    .then_inc(s_hts, 1)

            def store_y(j, k, saved):
                dve.wait_ge(s_yf, j + 1)
                if saved is not None:
                    dve.wait_ge(s_ysv[k], 16 * saved)
                nc.vector.tensor_copy(y_sb[:, k, :], ps[6 + k][:]).then_inc(s_ys, 1)

            hidden(0, 0, True)
            hidden(1, 1, True)
            store_hidden(0, 0, True)
            for j in (2, 3):
                hidden(j, j % 2, False)
                store_hidden(j - 1, (j - 1) % 2, j < 3)
                store_y(j - 2, j % 2, None)
            with dve.Fori(2, NS // 2) as i:
                for k in range(2):
                    hidden(2 * i + k, k, False)
                    store_hidden(2 * i + k - 1, 1 - k, False)
                    store_y(2 * i + k - 2, k, i - 1)
            hidden(NS - 1, 0, False)
            store_hidden(NS - 2, 1, False)
            store_y(NS - 3, 0, (NS - 3) // 2)
            store_hidden(NS - 1, 0, False)
            store_y(NS - 2, 1, (NS - 2) // 2)
            store_y(NS - 1, 0, (NS - 1) // 2)

            for t in range(NT):
                k = t % 4
                dve.wait_ge(s_ya[k], 32 * (t // 4 + 1))
                nc.vector.scalar_tensor_tensor(out=ya[:, k, :], in0=ya[:, k, :], scalar=prob[:, 0, t:t + 1],
                                               in1=rows[:, t, :], op0=ALU.mult, op1=ALU.add).then_inc(s_c1, 1)
                dve.wait_ge(s_c1, t + 1)
                nc.vector.scalar_tensor_tensor(out=ya[:, k, :], in0=yb[:, k, :], scalar=prob[:, 1, t:t + 1],
                                               in1=ya[:, k, :], op0=ALU.mult, op1=ALU.add).then_inc(s_c2, 1)

        @block.tensor
        def _(pe):
            pe.wait_ge(s_const, 13)

            def free_pj(b, key):
                n = pj_at[key]
                if n >= 3:
                    kind, i = pj_order[n - 3]
                    s, per, place = PJ_STORE[kind]
                    pe.wait_ge(s, b * per + place(i))

            def transpose_tile(b, key, src):
                n = tp_at[key]
                if n >= 2:
                    pe.wait_ge(s_tpst, b * NTP + n - 1)
                for c in range(C):
                    last = nc.tensor.transpose(tp_bank(key)[:, c * P:(c + 1) * P], src[:, c * P:(c + 1) * P], ident[:])
                last.then_inc(s_tp, 1)

            def stored(b, key):
                pe.wait_ge(s_tpst, b * NTP + tp_at[key] + 1)

            def project(b, key, w, lhs, filled):
                free_pj(b, key)
                for c in range(C):
                    last = nc.tensor.matmul(pj_bank(key)[:], lhs(c), w(c), start=(c == 0), stop=(c == C - 1))
                last.then_inc(filled, 1)

            def state(b, i):
                pe.wait_ge(s_kvs, b * 2 * TB + 2 * i + 2)
                for c in range(C):
                    last = nc.tensor.matmul(kv_ps[:, c * P:(c + 1) * P], k_sb[:, i % 2, c * P:(c + 1) * P],
                                            v_sb[:, i % 2, c * P:(c + 1) * P], start=(i == 0 and c == 0),
                                            stop=(i == TB - 1 and c == C - 1), skip_group_check=True)
                last.then_inc(s_kvused, 1)

            with pe.Fori(0, B) as b:
                for t in range(BLK):
                    pe.wait_ge(s_xn, b * TB + t + 1)
                    transpose_tile(b, ("x", t), xn[:, t % 2, :])
                for i in range(TB):
                    g, o = i // BLK, (i % BLK) * P
                    stored(b, ("x", i))
                    for n, (name, filled) in enumerate((("k", s_kvf), ("v", s_kvf), ("u", s_uf))):
                        pe.wait_ge(s_w[n + 1], 16)
                        project(b, (name, i), lambda c, n=n: w_attn[:, n + 1, c, :],
                                lambda c: xT[:, g, c, o:o + P], filled)
                        if name == "k" and i > 0:
                            state(b, i - 1)
                    if i + BLK < TB:
                        pe.wait_ge(s_xn, b * TB + i + BLK + 1)
                        transpose_tile(b, ("x", i + BLK), xn[:, i % 2, :])
                    if i % BLK == BLK - 1:
                        pe.wait_ge(s_w[0], 16)
                        for m in range(C):
                            project(b, ("q", g * C + m), lambda c: xT[:, g, c, :],
                                    lambda c, m=m: w_attn[:, 0, c, m * P:(m + 1) * P], s_qf)
                state(b, TB - 1)
                pe.wait_ge(s_qs, b * NB * C + NB * C)
                pe.wait_ge(s_sts, b * (1 + G) + 1 + G)
                for s in range(STEPS_B):
                    if s < TB:
                        if s >= 2:
                            pe.wait_ge(s_a1, b * TB + s - 1)
                        for c in range(C):
                            last = nc.tensor.matmul(o_ps[s % 2][:, c * P:(c + 1) * P], qT[:, c, s * P:(s + 1) * P],
                                                    kv_bd[:, c, :], start=True, stop=True)
                        last.then_inc(s_of, 1)
                    if 2 <= s < TB + 2:
                        j = s - 2
                        pe.wait_ge(s_att, b * TB + j + 1)
                        transpose_tile(b, ("a", j), att[:, j % 2, :])
                        stored(b, ("a", j))
                        pe.wait_ge(s_w[4], 16)
                        project(b, ("p", j), lambda c: w_o[:, c, :], lambda c: attT[:, j % 2, c, :], s_pf)
                    if 4 <= s < TB + 4:
                        j = s - 4
                        pe.wait_ge(s_h, b * TB + j + 1)
                        transpose_tile(b, ("h", j), h_sb[:, j % 2, :])
                    if 5 <= s < TB + 5:
                        j = s - 5
                        stored(b, ("h", j))
                        pe.wait_ge(s_wr, 16)
                        free_pj(b, ("r", j))
                        for c in range(C):
                            last = nc.tensor.matmul(pj_bank(("r", j))[:, 0:E], hT[:, j % 2, c, :], w_r[:, c, :],
                                                    start=(c == 0), stop=(c == C - 1))
                        last.then_inc(s_rf, 1)
                pe.wait_ge(s_tpst, (b + 1) * NTP)
                pe.wait_ge(s_x1, (b + 1) * TB)
                pe.wait_ge(s_sc, (b + 1) * TB)

            pe.wait_ge(s_v, MASK_MADE)
            m2 = mask[:].rearrange("p t e -> p (t e)")
            nc.tensor.matmul(ps[0][:, 0:NT * E], tri[:], m2, start=True, stop=True)
            for t in range(1, NT):
                nc.tensor.matmul(ps[0][:, t * E:NT * E], ones[:], m2[:, 0:(NT - t) * E], start=False,
                                 stop=True, skip_group_check=True)
            for t in range(NT):
                last = nc.tensor.matmul(ps[1][:, 0:E], ones[:], mask[:, t, :], start=(t == 0), stop=(t == NT - 1))
            last.then_inc(s_cnt, 1)
            pe.wait_ge(s_v, IDS_MADE)
            for r in range(R2):
                last = nc.tensor.matmul(ps[2][:, 0:2 * NS], hit_lo[:, r, :],
                                        id_hi[:, r, :, :].rearrange("p a s -> p (a s)"),
                                        start=(r == 0), stop=(r == R2 - 1))
            last.then_inc(s_tok, 1)

            def transpose_slots(j, k, gathers, first):
                pe.wait_ge(s_xg[k], 16 * gathers)
                if not first:
                    pe.wait_ge(s_xgs, j - 1)
                for c in range(C):
                    last = nc.tensor.transpose(ps[k][:, c * P:(c + 1) * P], xg[:, k, c * P:(c + 1) * P], ident[:])
                last.then_inc(s_xgt, 1)

            def gate_up(j, k, first):
                e = pe.value_load(expert[0:1, bass.ds(j, 1)], min_val=0, max_val=E - 1)
                pe.wait_ge(s_xgs, j + 1)
                if not first:
                    pe.wait_ge(s_hid, j - 1)
                for c in range(C):
                    last = nc.tensor.matmul(ps[2 + k][:, 0:2 * F], xgT[:, k, c, :],
                                            w_gu[:, bass.ds(e, 1), c * 2 * F:(c + 1) * 2 * F]
                                            .rearrange("p a n -> p (a n)"),
                                            start=(c == 0), stop=(c == C - 1))
                last.then_inc(s_guf, 1)

            def transpose_hidden(j, k, first):
                pe.wait_ge(s_hid, j + 1)
                if not first:
                    pe.wait_ge(s_hts, j - 1)
                for c in range(FH):
                    last = nc.tensor.transpose(ps[4 + k][0:FP, c * P:(c + 1) * P], hid[:, k, c * FP:(c + 1) * FP],
                                               ident[:])
                last.then_inc(s_ht, 1)

            def down(j, k, first):
                e = pe.value_load(expert[0:1, bass.ds(j, 1)], min_val=0, max_val=E - 1)
                pe.wait_ge(s_hts, j + 1)
                if not first:
                    pe.wait_ge(s_ys, j - 1)
                for c in range(FH):
                    last = nc.tensor.matmul(ps[6 + k][:], hidT[0:FP, k, c, :],
                                            w_dn[:, bass.ds(e, 1), c * D:(c + 1) * D]
                                            .rearrange("p a n -> p (a n)"),
                                            start=(c == 0), stop=(c == FH - 1))
                last.then_inc(s_yf, 1)

            pe.wait_ge(s_route, 1)
            pe.wait_ge(s_wgu, 16)
            transpose_slots(0, 0, 1, True)
            gate_up(0, 0, True)
            transpose_slots(1, 1, 1, True)
            gate_up(1, 1, True)
            transpose_hidden(0, 0, True)
            transpose_slots(2, 0, 2, False)
            pe.wait_ge(s_wdn, 16)
            for j in (2, 3):
                gate_up(j, j % 2, False)
                transpose_hidden(j - 1, 1 - j % 2, j < 3)
                transpose_slots(j + 1, 1 - j % 2, (j + 1) // 2 + 1, False)
                down(j - 2, j % 2, True)
            with pe.Fori(2, NS // 2) as i:
                gate_up(2 * i, 0, False)
                transpose_hidden(2 * i - 1, 1, False)
                transpose_slots(2 * i + 1, 1, i + 1, False)
                down(2 * i - 2, 0, False)
                gate_up(2 * i + 1, 1, False)
                transpose_hidden(2 * i, 0, False)
                transpose_slots(2 * i + 2, 0, i + 2, False)
                down(2 * i - 1, 1, False)
            gate_up(NS - 1, 0, False)
            transpose_hidden(NS - 2, 1, False)
            down(NS - 3, 0, False)
            transpose_hidden(NS - 1, 0, False)
            down(NS - 2, 1, False)
            down(NS - 1, 0, False)


def kernel(**inputs):
    import numpy as np
    import concourse.bacc as bacc
    from concourse.bass_utils import run_bass_kernel_spmd

    def at(name):
        return np.asarray(inputs["L0_" + name])

    def chunks(w):
        return w.T.reshape(C, P, w.shape[0]).transpose(1, 0, 2)

    x = at("attn_x")
    T = x.shape[0] * x.shape[1]
    slots = (2 * T + E * (P - 1)) // P * P
    gate, up, dn = at("ffn_w_gate_proj"), at("ffn_w_up_proj"), at("ffn_w_down_proj")
    gateup = np.concatenate([gate, up], axis=1)
    arrays = {
        "x": x.reshape(T, D),
        "wqkvu": np.stack([chunks(at("attn_" + n)) for n in ("wq", "wk", "wv", "wu")]),
        "wo": chunks(at("attn_wo")),
        "wrouter": chunks(at("ffn_w_gate_router")),
        "wgateup": np.stack([chunks(gateup[e]) for e in range(E)], axis=1).reshape(P, E, C * 2 * F),
        "wdown": dn.transpose(0, 2, 1).reshape(E, FH, FP, D).transpose(2, 0, 1, 3).reshape(FP, E, FH * D),
    }
    arrays = {k: np.ascontiguousarray(v) for k, v in arrays.items()}
    nc = bacc.Bacc("TRN2", target_bir_lowering=False, num_devices=1)
    args = {k: nc.dram_tensor("in_" + k, v.shape, mybir.dt.from_np(v.dtype), kind="ExternalInput").ap()
            for k, v in arrays.items()}
    h_dram = nc.dram_tensor("h_rows", (T, D), F32, kind="Internal").ap()
    y_dram = nc.dram_tensor("y_rows", (slots, D), F32, kind="Internal").ap()
    out = nc.dram_tensor("out", (T, D), F32, kind="ExternalOutput").ap()
    attention_and_moe(nc, h_dram=h_dram, y_dram=y_dram, out=out, **args)
    r = run_bass_kernel_spmd(nc, [{"in_" + k: v for k, v in arrays.items()}], core_ids=[0])
    return r.results[0]["out"].reshape(x.shape)
```

```python
from contextlib import ExitStack

import concourse.bass as bass
from concourse import mybir

ALU = mybir.AluOpType
ACT = mybir.ActivationFunctionType
F32 = mybir.dt.float32
F32R = mybir.dt.float32r
BF16 = mybir.dt.bfloat16
I32 = mybir.dt.int32
U32 = mybir.dt.uint32
AX_X = mybir.AxisListType.X

P = 128
D = 512
C = D // P
HD = 32
H = D // HD
G = P // HD
E = 8
F = 192
FB = F - P
GU = C * 2 * F
WE = GU + 2 * D
WL = GU + D
PIECES = 4
PIECE = WE // PIECES
EPS = 1e-5


def attention_and_moe(nc, x, wqkvuo, wrouter, wexperts, h_dram, out):
    T = x.shape[0]
    B = 2
    L = T // B
    NT = T // P
    TB = L // P
    BLK = 4
    NB = TB // BLK
    NS = (2 * T + E * (P - 1)) // P
    NE = NS + NS % 2
    R2 = 2 * NT
    PT = NT // 2
    NW = 5
    XB = 3
    EB = 6
    STEPS = NT + 2
    EARLY = 18
    HI, LO = 0, 1


    with ExitStack() as ctx:
        def sb(name, shape, dt=F32):
            return ctx.enter_context(nc.sbuf_tensor(name, shape, dt))

        def sem(name):
            return ctx.enter_context(nc.semaphore(name))

        class Arena:

            def __init__(self, name, size, dt):
                self.t, self.size, self.at = sb(name, [P, size], dt), size, 0

            def take(self, *shape):
                n = 1
                for d in shape:
                    n *= d
                a, self.at = self.at, self.at + n
                assert self.at <= self.size, (self.at, self.size)
                v = self.t[:, a:self.at]
                names = "abcde"[:len(shape)]
                if len(shape) > 1:
                    v = v.rearrange(f"p ({' '.join(names)}) -> p {' '.join(names)}",
                                    **{m: d for m, d in zip(names[1:], shape[1:])})
                return v

        parts = Arena("parts", NW * 2 * C * D + 2 * C * L + 2 * C * BLK * P + 2 * 2 * 2 * D + 2 * C * P + 2 * 2 * C * P,
                      F32R)
        wk, wv = parts.take(2, C * D), parts.take(2, C * D)
        k_sb = parts.take(2, 2, D)
        v_sb = parts.take(2, 2, D)
        wq = parts.take(2, C * D)
        xT = parts.take(2, C, L)
        wu = parts.take(2, C * D)
        qT = parts.take(2, C, BLK * P)
        kv_bd = parts.take(2, C, P)
        wo = parts.take(2, C * D)
        attT = parts.take(2, 2, C, P)
        parts.at = 0
        w_ex = parts.take(E, WE + WL)
        xgT = parts.take(2, 2, C, P)
        hidT = parts.take(2, 2, 2, P)
        LATE = (E - 1) * PIECES
        parts.at = (E - 1) * (WE + WL)
        places = parts.take(3, PT, P)
        id_hi = parts.take(R2, 3, NE)
        prob_hi = parts.take(2, NT)

        rows = Arena("rows", 11520, F32)
        x_in = rows.take(XB, D)
        xn = rows.take(2, D)
        rows.at = 0
        e_raw = rows.take(EB, PIECE)
        slots_at = rows.at
        x_res = rows.take(2, D)
        x1 = rows.take(2, D)
        sq = rows.take(2, D)
        stage_at = rows.at
        att = rows.take(2, D)
        u = rows.take(2, D)
        h_sb = rows.take(2, D)
        hT = rows.take(2, C, P)
        zero = rows.take(D)
        rows.at = stage_at
        w_raw = rows.take(2, C * D)
        rows.at = slots_at
        xg = rows.take(2, D)
        sg = rows.take(2, F)
        hid = rows.take(2, 2 * P)
        y_sb = rows.take(2, D)
        rows.at = slots_at
        hot = [rows.take(NT, E) for _ in range(2)]
        slot_all = rows.take(NT, E)
        picked = rows.take(NT, E)
        above = rows.take(E, NT)
        before = rows.take(NS, E)
        hit_hi = rows.take(R2, NE)
        top_idf, slotf = rows.take(2, NT), rows.take(2, NT)
        found = rows.take(3, NE)
        spare_f, expert_f, start_f, start2 = [rows.take(NS) for _ in range(4)]
        lo_f, hi_f = rows.take(R2), rows.take(R2)

        w_r = sb("w_r", [P, C, E])
        ident = sb("ident", [P, P])
        expo = sb("expo", [P, H])
        bstat = sb("bstat", [P, 6])
        mv = sb("mv", [P, 4, 2])
        rstd = sb("rstd", [P, 4])
        ss = sb("ss", [P, 2, H])
        rn = sb("rn", [P, 2, H])
        rn_in = sb("rn_in", [P, H])
        scores = sb("scores", [P, NT, E])
        top = sb("top", [P, NT, E])
        top_id = sb("top_id", [P, NT, E], U32)
        mask = sb("mask", [P, NT, E], BF16)
        iota_e = sb("iota_e", [P, E])
        iota_lo = sb("iota_lo", [P, P])
        thresh = sb("thresh", [P, NT])
        upto = sb("upto", [P, E, E])
        js = sb("js", [P, NE])
        nums = sb("nums", [P, 4, E])
        slot = sb("slot", [P, 2, NT], I32)
        lo_i = sb("lo_i", [P, 2, NT], I32)
        hi_i = sb("hi_i", [P, 2, NT], I32)
        id1 = sb("id1", [P, NT])
        spare = sb("spare", [P, 1])
        tri = sb("tri", [P, P], BF16)
        ones = sb("ones", [P, P], BF16)
        tok_w = sb("tok_w", [P, 2, NS])
        token = sb("token", [P, NS], U32)
        expert = sb("expert", [P, NS], I32)
        start_i = sb("start_i", [P, NS], I32)
        adds = sb("adds", [P, 2, NS], I32)
        pick = sb("pick", [P, 2], U32)
        put = sb("put", [P, 2], U32)
        gap = sb("gap", [P, NT])
        egap = sb("egap", [P, NT])
        prob = sb("prob", [P, 2, NT])
        prob_lo = sb("prob_lo", [P, 2, NT])

        ps = [ctx.enter_context(nc.psum_tensor(f"ps{i}", [P, 512], F32)) for i in range(8)]
        tp = ps[0:2]
        pj = ps[2:5]
        kv_ps = ps[5]
        o_ps = ps[6:8]

        s_wk = [sem(f"wk_loaded{c}") for c in range(C)]
        s_w = {n: sem(f"w{n}_loaded") for n in "qvuo"}
        s_wr = sem("router_loaded")
        s_x = [sem(f"x_loaded{i}") for i in range(XB)]
        s_xr = [sem(f"x_reloaded{i}") for i in range(2)]
        s_er = [sem(f"experts_loaded{i}") for i in range(EB)]
        s_x1sv = [sem(f"x1_saved{i}") for i in range(2)]
        s_hsv = [sem(f"h_saved{i}") for i in range(2)]
        s_const = sem("constants_made")
        s_whi, s_wlo = sem("weight_hi_made"), sem("weight_lo_made")
        s_ehi, s_elo, s_elop = sem("expert_hi_made"), sem("expert_lo_made"), sem("expert_lo_made_by_pool")
        s_bst, s_var = sem("stats_made"), sem("var_made")
        s_rsi, s_rstd = sem("rstd_base_made"), sem("rstd_made")
        s_xn, s_h = sem("xn_made"), sem("h_made")
        s_xf, s_xhi, s_xlo = sem("x_transposed"), sem("xT_hi_stored"), sem("xT_lo_stored")
        s_kvf, s_kvhi, s_kvlo = sem("k_or_v_filled"), sem("k_or_v_hi_stored"), sem("k_or_v_lo_stored")
        s_kvused, s_st, s_stlo = sem("kv_used"), sem("state_hi_stored"), sem("state_lo_stored")
        s_qf, s_qhi, s_qlo = sem("q_filled"), sem("q_hi_stored"), sem("q_lo_stored")
        s_uf, s_us = sem("u_filled"), sem("u_stored")
        s_of, s_sq, s_ss = sem("o_filled"), sem("squares_made"), sem("square_sums_made")
        s_rni, s_rn = sem("norm_base_made"), sem("norm_made")
        s_a1, s_att = sem("normed"), sem("gated")
        s_af, s_ahi, s_alo = sem("att_transposed"), sem("attT_hi_stored"), sem("attT_lo_stored")
        s_pf, s_x1 = sem("attn_out_filled"), sem("x1_made")
        s_hf, s_hst = sem("h_transposed"), sem("hT_stored")
        s_rf, s_sc = sem("scores_filled"), sem("scores_stored")
        s_top, s_topid = sem("top_scores_made"), sem("top_ids_made")
        GAP_MADE, MASK_MADE, TILES_MADE, ROWS_MADE = 1, 4, 25, 26
        s_v = sem("routing_step")
        s_second = sem("second_rows_made")
        s_cnt, s_eg, s_tok, s_route = sem("ranks_filled"), sem("exp_made"), sem("tokens_filled"), sem("routing_made")
        s_pick, s_put = sem("pick_made"), sem("put_made")
        s_xg = [sem(f"gathered{i}") for i in range(2)]
        s_xgt, s_xghi, s_xglo = sem("slots_transposed"), sem("slots_hi_stored"), sem("slots_lo_stored")
        s_guf, s_sg, s_hid = sem("gateup_filled"), sem("silu_made"), sem("hidden_made")
        s_ht, s_hthi, s_htlo = sem("hidden_transposed"), sem("hidden_hi_stored"), sem("hidden_lo_stored")
        s_yf, s_ys = sem("y_filled"), sem("y_stored")
        s_add = [sem(f"added{i}") for i in range(2)]

        tp_order = [("x", 0), ("x", 1)] + [("x", i + 2) for i in range(TB - 2)] + [("x", TB)]
        pj_order = [(name, i) for i in range(TB) for name in "kv"] + [("q", m) for m in range(C)] + [("u", 0)]
        ln_order = [("x", i) for i in range(TB + 2)]
        for s in range(STEPS):
            if 1 <= s < NT + 1:
                tp_order.append(("a", s - 1))
            if s + 1 < NT:
                pj_order.append(("u", s + 1))
            if s >= 2:
                tp_order.append(("h", s - 2))
            if TB + s < NT:
                pj_order += [("k", TB + s), ("v", TB + s)]
            if s < NT - 1 and s % BLK == BLK - 1:
                pj_order += [("q", (s // BLK + 1) * C + m) for m in range(C)]
            if TB + s + 1 < NT:
                tp_order.append(("x", TB + s + 1))
            if TB + s + 2 < NT:
                ln_order.append(("x", TB + s + 2))
            if 1 <= s < NT + 1:
                pj_order.append(("p", s - 1))
                ln_order.append(("y", s - 1))
            if s >= 2:
                pj_order.append(("r", s - 2))
        tp_at = {key: n for n, key in enumerate(tp_order)}
        pj_at = {key: n for n, key in enumerate(pj_order)}
        ln_at = {key: n for n, key in enumerate(ln_order)}
        LAST = {"x": (s_xlo, lambda i: i + 1), "a": (s_alo, lambda i: i + 1), "h": (s_hst, lambda i: i + 1),
                "k": (s_kvlo, lambda i: 2 * i + 1), "v": (s_kvlo, lambda i: 2 * i + 2),
                "u": (s_us, lambda i: i + 1), "q": (s_qlo, lambda i: i + 1),
                "p": (s_x1, lambda i: i + 1), "r": (s_sc, lambda i: i + 1)}

        def step_of(n):
            return TB + n // 2 + (1 if n >= 12 else 0)

        def by_pool(n):
            return n >= EARLY and n % PIECES != PIECES - 1 and n != LATE + 1

        def lo_count(pool):
            return sum(by_pool(n) == pool for n in range(E * PIECES))

        def lo_made(n):
            return (s_elop if by_pool(n) else s_elo), sum(by_pool(m) == by_pool(n) for m in range(n + 1))

        def place_free(n):
            e = n // PIECES
            if e < 2:
                return s_kvused, NT
            if e < 3:
                return s_qf, NT // BLK * C
            if e < 6:
                return s_uf, NT
            if n >= LATE:
                return s_tok, R2 // PT
            return s_pf, NT

        def tile_rows(engine, r):
            half = slice(r * NT, (r + 1) * NT)
            for a, factor in enumerate((id1[:], prob_hi[:, r, :].bitcast(F32), prob_lo[:, r, :])):
                last = engine.tensor_tensor(id_hi[:, half, a, :], hit_hi[:, half, :],
                                            factor.unsqueeze(2).to_broadcast([P, NT, NE]), ALU.mult)
            return last

        def one_hot_places(engine, n):
            return engine.tensor_tensor(places[:, n % 3], iota_lo[:].unsqueeze(1).to_broadcast([P, PT, P]),
                                        lo_f[:, n * PT:(n + 1) * PT].unsqueeze(2).to_broadcast([P, PT, P]),
                                        ALU.is_equal)

        def split_lo(eng, engine, n):
            e, c = n // PIECES, n % PIECES * PIECE
            width = max(0, min(PIECE, WL - c))
            eng.wait_ge(s_ehi, n + 1)
            ins = engine.tensor_tensor(w_ex[:, e, WE + c:WE + c + width], e_raw[:, n % EB, 0:width],
                                       w_ex[:, e, c:c + width].bitcast(F32), ALU.subtract)
            if width < PIECE:
                ins = engine.tensor_tensor(w_ex[FB:P, e, WL:WE], e_raw[FB:P, n % EB, width:PIECE],
                                           w_ex[FB:P, e, WL:WE].bitcast(F32), ALU.subtract)
            ins.then_inc(s_elop if by_pool(n) else s_elo, 1)

        def ln_buffer(key):
            return key[1] % 2 + (2 if key[0] == "y" else 0)

        def bank(key):
            return tp[tp_at[key] % 2] if key in tp_at else pj[pj_at[key] % 3]

        def chunked(ap):
            return ap.rearrange("p (c n) -> p c n", c=C)

        block = ctx.enter_context(nc.Block())

        @block.sync
        def _(sp):
            def load_x(t):
                if t >= XB:
                    sp.wait_ge(s_xn, t - XB + 1)
                sp.dma_start(x_in[:, t % XB, :], x[t * P:(t + 1) * P, :]).then_inc(s_x[t % XB], 16)

            def reload_x(t):
                if t >= 2:
                    sp.wait_ge(s_x1, t - 1)
                sp.dma_start(x_res[:, t % 2, :], x[t * P:(t + 1) * P, :]).then_inc(s_xr[t % 2], 16)

            def load_weight(name, at, k, split):
                if split:
                    sp.wait_ge(s_wlo, split)
                sp.dma_start(w_raw[:, k, :], wqkvuo[at]).then_inc(s_w[name], 16)

            def load_piece(n):
                if n >= EB:
                    sp.wait_ge(*lo_made(n - EB))
                else:
                    sp.wait_ge(s_xf, NT)
                sp.dma_start(e_raw[:, n % EB, :], wexperts[n // PIECES, :, n % PIECES * PIECE:(n % PIECES + 1) * PIECE])\
                    .then_inc(s_er[n % EB], 16)

            load_x(0)
            load_x(1)
            for c in range(C):
                sp.dma_start(w_raw[:, 0, c * D:(c + 1) * D], wqkvuo[1, :, c * D:(c + 1) * D]).then_inc(s_wk[c], 16)
            load_weight("v", 2, 1, 0)
            for t in range(2, 5):
                load_x(t)
            for i in range(TB):
                if i == 0:
                    load_weight("q", 0, 0, C)
                if i == 1:
                    load_weight("u", 3, 1, C + 1)
                if i == 2:
                    load_weight("o", 4, 0, C + 2)
                    sp.dma_start(w_r[:], wrouter).then_inc(s_wr, 16)
                if i + 5 < TB + XB:
                    load_x(i + 5)
            reload_x(0)
            reload_x(1)
            load_x(TB + XB)
            for s in range(STEPS):
                if s >= 2:
                    sp.wait_ge(s_h, s - 1)
                    sp.dma_start(h_dram[(s - 2) * P:(s - 1) * P, :], h_sb[:, s % 2, :]).then_inc(s_hsv[s % 2], 16)
                if TB + XB + 1 + s < NT:
                    load_x(TB + XB + 1 + s)
                for n in range(E * PIECES):
                    if n < EARLY and step_of(n) == s + 1:
                        load_piece(n)
                if 1 <= s < NT + 1:
                    j = s - 1
                    sp.wait_ge(s_x1, s)
                    sp.dma_start(out[j * P:s * P, :], x1[:, j % 2, :]).then_inc(s_x1sv[j % 2], 16)
                    if s + 1 < NT:
                        reload_x(s + 1)
            for n in range(EARLY, E * PIECES):
                load_piece(n)
            for k in range(2):
                sp.wait_ge(s_add[k], 16 * (1 + (NS + 1 - k) // 2))

        @block.gpsimd
        def _(pool):
            def made(ins):
                ins.then_inc(s_const, 1)

            def iota(ap, pattern, base=0, channel=0):
                made(nc.gpsimd.iota(ap, pattern=pattern, base=base, channel_multiplier=channel,
                                    allow_small_or_imprecise_dtypes=True))

            made(nc.gpsimd.memset(ident[:], 0.0))
            made(nc.gpsimd.memset(expo[:], -0.5))
            pool.wait_ge(s_const, 2)
            made(nc.gpsimd.affine_select(out=ident[:], in_=ident[:], compare_op=ALU.not_equal, fill=1.0,
                                         base=0, pattern=[[-1, P]], channel_multiplier=1))
            made(nc.gpsimd.memset(tri[:], 0.0))
            made(nc.gpsimd.memset(ones[:], 1.0))
            made(nc.gpsimd.memset(upto[:], 1.0))
            made(nc.gpsimd.memset(zero, 0.0))
            pool.wait_ge(s_const, 7)
            made(nc.gpsimd.affine_select(out=tri[:], in_=tri[:], compare_op=ALU.is_ge, fill=1.0,
                                         base=0, pattern=[[-1, P]], channel_multiplier=1))
            made(nc.gpsimd.affine_select(out=upto[:], in_=upto[:], compare_op=ALU.is_ge, fill=0.0,
                                         base=0, pattern=[[1, E], [-1, E]], channel_multiplier=0))
            iota(id1[:], [[P, NT]], base=1, channel=1)
            iota(spare[:], [[0, 1]], base=T + 1, channel=1)
            iota(iota_e[:], [[1, E]])
            iota(iota_lo[:], [[1, P]])
            iota(thresh[:], [[P, NT]])
            iota(js[:], [[1, NE]])
            nc.gpsimd.dma_start(h_dram[T:T + P, :], zero).then_inc(s_add[0], 16)
            nc.gpsimd.dma_start(out[T:T + P, :], zero).then_inc(s_add[1], 16)

            def inverse_deviation(n, k):
                pool.wait_ge(s_rsi, n)
                nc.gpsimd.tensor_tensor(rstd[:, k:k + 1], rstd[:, k:k + 1], expo[:, 0:1], ALU.pow).then_inc(s_rstd, 1)

            for i in range(TB + 2):
                inverse_deviation(i + 1, ln_buffer(("x", i)))
            for s in range(STEPS):
                if s < NT:
                    pool.wait_ge(s_ss, s + 1)
                    nc.gpsimd.tensor_scalar(rn_in[:], ss[:, s % 2, :], 1e-24, float(HD * HD), ALU.max, ALU.mult)\
                        .then_inc(s_rni, 1)
                    pool.wait_ge(s_rni, s + 1)
                    nc.gpsimd.tensor_tensor(rn[:, s % 2, :], rn_in[:], expo[:], ALU.pow).then_inc(s_rn, 1)
                if TB + s + 2 < NT:
                    inverse_deviation(ln_at["x", TB + s + 2] + 1, ln_buffer(("x", TB + s + 2)))
                if 1 <= s < NT + 1:
                    inverse_deviation(ln_at["y", s - 1] + 1, ln_buffer(("y", s - 1)))

            for n in range(EARLY, LATE):
                if by_pool(n):
                    split_lo(pool, nc.gpsimd, n)
            pool.wait_ge(s_v, TILES_MADE)
            tile_rows(nc.gpsimd, 1).then_inc(s_second, 1)

            def gather(j, k, gathered, transposed):
                if gathered is not None:
                    pool.wait_ge(s_xg[k], 16 * gathered)
                if transposed is not None:
                    pool.wait_ge(s_xgt, transposed)
                nc.gpsimd.tensor_copy(pick[:, k:k + 1], token[:, bass.ds(j, 1)]).then_inc(s_pick, 1)
                pool.wait_ge(s_pick, j + 1)
                pool.nop(nofuse=True)
                nc.gpsimd.indirect_dma_start(
                    out=xg[:, k, :], out_offset=None, in_=h_dram,
                    in_offset=bass.IndirectOffsetOnAxis(ap=pick[:, k:k + 1], axis=0)).then_inc(s_xg[k], 16)

            def add(j, k, before):
                if before is not None:
                    pool.wait_ge(s_add[k], 16 * before)
                need = [pool.value_load(adds[0:1, r, bass.ds(j, 1)], min_val=16, max_val=16 * (NS + 1))
                        for r in range(2)]
                nc.gpsimd.tensor_copy(put[:, k:k + 1], token[:, bass.ds(j, 1)]).then_inc(s_put, 1)
                for r in range(2):
                    pool.wait_ge(s_add[r], need[r])
                pool.wait_ge(s_ys, j + 1)
                pool.wait_ge(s_put, j + 1)
                pool.nop(nofuse=True)
                nc.gpsimd.indirect_dma_start(
                    out=out, out_offset=bass.IndirectOffsetOnAxis(ap=put[:, k:k + 1], axis=0),
                    in_=y_sb[:, k, :], in_offset=None, compute_op=ALU.add).then_inc(s_add[k], 16)

            pool.wait_ge(s_route, 1)
            for k in range(2):
                pool.wait_ge(s_hsv[k], 16 * (NT // 2))
                pool.wait_ge(s_x1sv[k], 16 * (NT // 2))
                pool.wait_ge(s_add[k], 16)
            gather(0, 0, None, None)
            gather(1, 1, None, None)
            for n in range(LATE, E * PIECES):
                if by_pool(n):
                    split_lo(pool, nc.gpsimd, n)
            for j in range(2, 6):
                gather(j, j % 2, j // 2, j - 1)
            with pool.Fori(1, (NS - 5) // 2) as i:
                for k in range(2):
                    gather(2 * i + k + 4, k, i + 2, 2 * i + k + 3)
                    add(2 * i + k - 2, k, i)
            gather(NS - 1, 0, (NS - 1) // 2, NS - 2)
            for j in range(NS - 7, NS):
                add(j, j % 2, j // 2 + 1)

        @block.scalar
        def _(act):
            def weight_hi(name, dst, k):
                act.wait_ge(s_w[name], 16)
                nc.scalar.activation(dst[:, HI, :], w_raw[:, k, :], ACT.Copy).then_inc(s_whi, 1)

            def hi(filled, count, dst, key, func, done, shaped=True):
                act.wait_ge(filled, count)
                src = bank(key)[:]
                nc.scalar.activation(dst, chunked(src) if shaped else src, func).then_inc(done, 1)

            def x_hi(t):
                at = t % TB * P
                hi(s_xf, t + 1, xT[:, HI, :, at:at + P], ("x", t), ACT.Copy, s_xhi)

            def k_hi(t):
                if t >= 2:
                    act.wait_ge(s_kvused, t - 1)
                hi(s_kvf, 2 * t + 1, k_sb[:, t % 2, HI, :], ("k", t), ACT.Relu, s_kvhi, False)

            def v_hi(t):
                hi(s_kvf, 2 * t + 2, v_sb[:, t % 2, HI, :], ("v", t), ACT.Copy, s_kvhi, False)

            def q_hi(g):
                for m in range(C):
                    hi(s_qf, g * C + m + 1, qT[:, HI, m, :], ("q", g * C + m), ACT.Relu, s_qhi, False)

            def u_silu(t):
                if t >= 2:
                    act.wait_ge(s_att, t - 1)
                hi(s_uf, t + 1, u[:, t % 2, :], ("u", t), ACT.Silu, s_us, False)

            def expert_hi(n):
                e, c = n // PIECES, n % PIECES * PIECE
                act.wait_ge(s_er[n % EB], 16 * (n // EB + 1))
                act.wait_ge(*place_free(n))
                nc.scalar.activation(w_ex[:, e, c:c + PIECE], e_raw[:, n % EB, :], ACT.Copy).then_inc(s_ehi, 1)

            x_hi(0)
            x_hi(1)
            for c in range(C):
                act.wait_ge(s_wk[c], 16)
                nc.scalar.activation(wk[:, HI, c * D:(c + 1) * D], w_raw[:, 0, c * D:(c + 1) * D], ACT.Copy)\
                    .then_inc(s_whi, 1)
            weight_hi("v", wv, 1)
            for i in range(TB):
                k_hi(i)
                v_hi(i)
                if i + 2 < TB:
                    x_hi(i + 2)
                if i == 1:
                    weight_hi("q", wq, 0)
                if i == 2:
                    weight_hi("u", wu, 1)
                if i == 3:
                    weight_hi("o", wo, 0)
            q_hi(0)
            u_silu(0)
            x_hi(TB)
            for s in range(STEPS):
                if s < NT:
                    act.wait_ge(s_of, s + 1)
                    if s >= 2:
                        act.wait_ge(s_ss, s - 1)
                    nc.scalar.activation(sq[:, s % 2, :], o_ps[s % 2][:], ACT.Square,
                                         scale=1.0 / (HD * HD ** 0.5)).then_inc(s_sq, 1)
                if 1 <= s < NT + 1:
                    j = s - 1
                    if j >= 2:
                        act.wait_ge(s_pf, j - 1)
                    hi(s_af, j + 1, attT[:, j % 2, HI], ("a", j), ACT.Copy, s_ahi)
                for n in range(EARLY):
                    if step_of(n) == s:
                        expert_hi(n)
                if s + 1 < NT:
                    u_silu(s + 1)
                if s >= 2:
                    j = s - 2
                    if j >= 2:
                        act.wait_ge(s_rf, j - 1)
                    hi(s_hf, j + 1, hT[:, j % 2], ("h", j), ACT.Copy, s_hst)
                if TB + s < NT:
                    k_hi(TB + s)
                    v_hi(TB + s)
                if s < NT - 1 and s % BLK == BLK - 1:
                    q_hi(s // BLK + 1)
                if TB + s + 1 < NT:
                    x_hi(TB + s + 1)

            act.wait_ge(s_v, GAP_MADE)
            nc.scalar.activation(egap[:], gap[:], ACT.Exp).then_inc(s_eg, 1)
            for n in range(EARLY, E * PIECES):
                expert_hi(n)

            def slots_hi(j, k):
                act.wait_ge(s_xgt, j + 1)
                nc.scalar.activation(xgT[:, k, HI], chunked(ps[k][:]), ACT.Copy).then_inc(s_xghi, 1)

            def silu(j, k):
                act.wait_ge(s_guf, j + 1)
                nc.scalar.activation(sg[:, k, :], ps[2 + k][:, 0:F], ACT.Silu).then_inc(s_sg, 1)

            def hidden_hi(j, k):
                act.wait_ge(s_ht, j + 1)
                nc.scalar.activation(hidT[:, k, HI], ps[4 + k][:, 0:2 * P].rearrange("p (c n) -> p c n", c=2), ACT.Copy)\
                    .then_inc(s_hthi, 1)

            def store_y(j, k, added):
                act.wait_ge(s_yf, j + 1)
                if added is not None:
                    act.wait_ge(s_add[k], 16 * added)
                nc.scalar.activation(y_sb[:, k, :], ps[6 + k][:], ACT.Copy, scale=tok_w[:, 1, bass.ds(j, 1)])\
                    .then_inc(s_ys, 1)

            act.wait_ge(s_route, 1)
            slots_hi(0, 0)
            slots_hi(1, 1)
            silu(0, 0)
            slots_hi(2, 0)
            silu(1, 1)
            hidden_hi(0, 0)
            slots_hi(3, 1)
            with act.Fori(1, (NS - 3) // 2) as i:
                for k in range(2):
                    silu(2 * i + k, k)
                    hidden_hi(2 * i + k - 1, 1 - k)
                    slots_hi(2 * i + k + 2, k)
                    store_y(2 * i + k - 2, k, i)
            for j in range(NS - 3, NS + 2):
                if j < NS:
                    silu(j, j % 2)
                if j - 1 < NS:
                    hidden_hi(j - 1, (j - 1) % 2)
                if j + 2 < NS:
                    slots_hi(j + 2, j % 2)
                store_y(j - 2, j % 2, (j - 2) // 2 + 1)

        @block.vector
        def _(dve):
            f32 = lambda ap: ap.bitcast(F32)

            nc.vector.memset(f32(kv_bd), 0.0).then_inc(s_st, 1)

            def weight_lo(n, w, k):
                dve.wait_ge(s_whi, C + n + 1)
                nc.vector.tensor_tensor(w[:, LO, :], w_raw[:, k, :], f32(w[:, HI, :]), ALU.subtract).then_inc(s_wlo, 1)

            def statistics(row, key):
                n, k = ln_at[key], ln_buffer(key)
                nc.vector.bn_stats(bstat[:], row).then_inc(s_bst, 1)
                dve.wait_ge(s_bst, n + 1)
                nc.vector.bn_aggr(mv[:, k, :], bstat[:]).then_inc(s_var, 1)
                dve.wait_ge(s_var, n + 1)
                nc.vector.tensor_scalar(rstd[:, k:k + 1], mv[:, k, 1:2], EPS, None, ALU.add).then_inc(s_rsi, 1)

            def normalised(dst, row, key, done):
                k = ln_buffer(key)
                dve.wait_ge(s_rstd, ln_at[key] + 1)
                nc.vector.tensor_scalar(dst, row, mv[:, k, 0:1], rstd[:, k:k + 1], ALU.subtract, ALU.mult)\
                    .then_inc(done, 1)

            def lo(his, count, dst, key, high, op, done, shaped=True):
                dve.wait_ge(his, count)
                src = chunked(bank(key)[:]) if shaped else bank(key)[:]
                if op is None:
                    nc.vector.tensor_tensor(dst, src, f32(high), ALU.subtract).then_inc(done, 1)
                else:
                    nc.vector.scalar_tensor_tensor(out=dst, in0=src, scalar=0.0, in1=f32(high), op0=op,
                                                   op1=ALU.subtract).then_inc(done, 1)

            def x_stats(t):
                dve.wait_ge(s_x[t % XB], 16 * (t // XB + 1))
                statistics(x_in[:, t % XB, :], ("x", t))

            def x_norm(t):
                if t >= 2:
                    dve.wait_ge(s_xf, t - 1)
                normalised(xn[:, t % 2, :], x_in[:, t % XB, :], ("x", t), s_xn)

            def x_lo(t):
                at = t % TB * P
                lo(s_xhi, t + 1, xT[:, LO, :, at:at + P], ("x", t), xT[:, HI, :, at:at + P], None, s_xlo)

            def k_lo(t):
                lo(s_kvhi, 2 * t + 1, k_sb[:, t % 2, LO, :], ("k", t), k_sb[:, t % 2, HI, :], ALU.max, s_kvlo, False)

            def v_lo(t):
                lo(s_kvhi, 2 * t + 2, v_sb[:, t % 2, LO, :], ("v", t), v_sb[:, t % 2, HI, :], None, s_kvlo, False)

            def q_lo(g):
                for m in range(C):
                    lo(s_qhi, g * C + m + 1, qT[:, LO, m, :], ("q", g * C + m), qT[:, HI, m, :], ALU.max, s_qlo, False)

            def store_state(b):
                dve.wait_ge(s_kvused, (b + 1) * TB)
                if b:
                    dve.wait_ge(s_of, b * TB)
                dve.wait_ge(s_st, b * G + 1)
                for half, done in ((HI, s_st), (LO, s_stlo)):
                    for q in range(G):
                        rng = slice(q * HD, (q + 1) * HD)
                        src = chunked(kv_ps[rng, :])[:, :, rng]
                        if half == HI:
                            nc.vector.tensor_copy(kv_bd[rng, HI, :, rng], src).then_inc(s_st, 1)
                        else:
                            nc.vector.tensor_tensor(kv_bd[rng, LO, :, rng], src, f32(kv_bd[rng, HI, :, rng]),
                                                    ALU.subtract).then_inc(s_stlo, 1)
                    if half == HI:
                        dve.wait_ge(s_st, (b + 1) * G + 1)

            def store_scores(t):
                dve.wait_ge(s_rf, t + 1)
                nc.vector.tensor_copy(scores[:, t, :], bank(("r", t))[:, 0:E]).then_inc(s_sc, 1)

            def top_scores(t):
                dve.wait_ge(s_sc, t + 1)
                nc.vector.max(top[:, t, :], scores[:, t, :]).then_inc(s_top, 1)

            def top_ids(t):
                dve.wait_ge(s_top, t + 1)
                nc.vector.max_index(top_id[:, t, :], top[:, t, :], scores[:, t, :]).then_inc(s_topid, 1)

            x_stats(0)
            x_norm(0)
            x_stats(1)
            x_norm(1)
            x_lo(0)
            for c in range(C):
                part = slice(c * D, (c + 1) * D)
                dve.wait_ge(s_whi, c + 1)
                nc.vector.tensor_tensor(wk[:, LO, part], w_raw[:, 0, part], f32(wk[:, HI, part]), ALU.subtract)\
                    .then_inc(s_wlo, 1)
            x_lo(1)
            x_stats(2)
            weight_lo(0, wv, 1)
            for i in range(TB):
                k_lo(i)
                if i + 2 < TB:
                    x_norm(i + 2)
                if i + 3 < TB + 1:
                    x_stats(i + 3)
                v_lo(i)
                if i + 2 < TB:
                    x_lo(i + 2)
                if i == 1:
                    weight_lo(1, wq, 0)
                if i == 2:
                    weight_lo(2, wu, 1)
                if i == 3:
                    weight_lo(3, wo, 0)
            x_norm(TB)
            x_stats(TB + 1)
            store_state(0)
            q_lo(0)
            x_lo(TB)
            for s in range(STEPS):
                if s < NT:
                    dve.wait_ge(s_sq, s + 1)
                    nc.vector.tensor_reduce(ss[:, s % 2, :], sq[:, s % 2, :].rearrange("p (h e) -> p h e", e=HD),
                                            axis=AX_X, op=ALU.add).then_inc(s_ss, 1)
                if s >= 3:
                    store_scores(s - 3)
                if s >= 2:
                    j = s - 2
                    if j >= 2:
                        dve.wait_ge(s_hf, j - 1)
                        dve.wait_ge(s_hsv[j % 2], 16 * (j // 2))
                    normalised(h_sb[:, j % 2, :], x1[:, j % 2, :], ("y", j), s_h)
                if 1 <= s < NT + 1:
                    j = s - 1
                    lo(s_ahi, j + 1, attT[:, j % 2, LO], ("a", j), attT[:, j % 2, HI], None, s_alo)
                if s >= 4:
                    top_scores(s - 4)
                if s >= 5:
                    top_ids(s - 5)
                for n in range(EARLY):
                    if step_of(n) == s:
                        split_lo(dve, nc.vector, n)
                if s < NT:
                    dve.wait_ge(s_rn, s + 1)
                    if s >= 2:
                        dve.wait_ge(s_af, s - 1)
                    nc.vector.tensor_tensor(
                        att[:, s % 2, :].rearrange("p (h e) -> p h e", e=HD),
                        o_ps[s % 2][:].rearrange("p (h e) -> p h e", e=HD),
                        rn[:, s % 2, :].unsqueeze(2).to_broadcast([P, H, HD]), ALU.mult).then_inc(s_a1, 1)
                    dve.wait_ge(s_a1, s + 1)
                    dve.wait_ge(s_us, s + 1)
                    nc.vector.tensor_tensor(att[:, s % 2, :], att[:, s % 2, :], u[:, s % 2, :], ALU.mult)\
                        .then_inc(s_att, 1)
                if TB + s < NT:
                    k_lo(TB + s)
                    if TB + s + 1 < NT:
                        x_norm(TB + s + 1)
                    if TB + s + 2 < NT:
                        x_stats(TB + s + 2)
                    v_lo(TB + s)
                if s < NT - 1 and s % BLK == BLK - 1:
                    q_lo(s // BLK + 1)
                if TB + s + 1 < NT:
                    x_lo(TB + s + 1)
                if s == TB - 1:
                    store_state(1)
                if 1 <= s < NT + 1:
                    j = s - 1
                    dve.wait_ge(s_pf, j + 1)
                    dve.wait_ge(s_xr[j % 2], 16 * (j // 2 + 1))
                    if j >= 2:
                        dve.wait_ge(s_x1sv[j % 2], 16 * (j // 2))
                    nc.vector.tensor_tensor(x1[:, j % 2, :], bank(("p", j))[:], x_res[:, j % 2, :], ALU.add)\
                        .then_inc(s_x1, 1)
                    dve.wait_ge(s_x1, j + 1)
                    statistics(x1[:, j % 2, :], ("y", j))
            store_scores(NT - 1)
            top_scores(NT - 2)
            top_scores(NT - 1)
            for t in range(NT - 3, NT):
                top_ids(t)
            for k in range(2):
                dve.wait_ge(s_x1sv[k], 16 * (NT // 2))
                dve.wait_ge(s_hsv[k], 16 * (NT // 2))

            steps = [0]

            def step(ins):
                steps[0] += 1
                ins.then_inc(s_v, 1)
                dve.wait_ge(s_v, steps[0])

            later = [n for n in range(EARLY, E * PIECES) if not by_pool(n)]

            def next_piece():
                split_lo(dve, nc.vector, later.pop(0))

            dve.wait_ge(s_const, 15)
            dve.wait_ge(s_top, NT)
            step(nc.vector.tensor_tensor(gap[:], top[:, :, 1], top[:, :, 0], ALU.subtract))
            assert steps[0] == GAP_MADE
            dve.wait_ge(s_topid, NT)
            step(nc.vector.tensor_copy(top_idf, top_id[:, :, 0:2].rearrange("p t r -> p r t")))
            dve.wait_ge(s_add[0], 16)
            dve.wait_ge(s_add[1], 16)
            for r in range(2):
                last = nc.vector.tensor_tensor(hot[r], iota_e[:].unsqueeze(1).to_broadcast([P, NT, E]),
                                               top_idf[:, r, :].unsqueeze(2).to_broadcast([P, NT, E]), ALU.is_equal)
            step(last)
            step(nc.vector.tensor_tensor(mask[:], hot[0], hot[1], ALU.add))
            assert steps[0] == MASK_MADE
            dve.wait_ge(s_eg, 1)
            step(nc.vector.tensor_scalar(gap[:], egap[:], 1.0, None, ALU.add))
            step(nc.vector.reciprocal(prob[:, 0, :], gap[:]))
            step(nc.vector.tensor_tensor(prob[:, 1, :], prob[:, 0, :], egap[:], ALU.mult))
            step(nc.vector.tensor_copy(prob_hi, prob[:]))
            step(nc.vector.tensor_tensor(prob_lo[:], prob[:], f32(prob_hi), ALU.subtract))
            next_piece()
            dve.wait_ge(s_cnt, 1)
            step(nc.vector.tensor_copy(nums[:, 0, :], ps[1][:, 0:E]))
            step(nc.vector.tensor_tensor(above, nums[:, 0, :].unsqueeze(2).to_broadcast([P, E, NT]),
                                         thresh[:].unsqueeze(1).to_broadcast([P, E, NT]), ALU.is_gt))
            step(nc.vector.tensor_reduce(nums[:, 1, :], above, axis=AX_X, op=ALU.add))
            step(nc.vector.tensor_tensor(before[:, 0:E, :], nums[:, 1, :].unsqueeze(1).to_broadcast([P, E, E]),
                                         upto[:], ALU.mult))
            step(nc.vector.tensor_reduce(nums[:, 2, :], before[:, 0:E, :], axis=AX_X, op=ALU.add))
            step(nc.vector.tensor_tensor(nums[:, 3, :], nums[:, 2, :], nums[:, 1, :], ALU.subtract))
            step(nc.vector.tensor_scalar(nums[:, 3, :], nums[:, 3, :], float(P), None, ALU.mult))
            step(nc.vector.tensor_tensor(slot_all, ps[0][:, 0:NT * E].rearrange("p (t e) -> p t e", t=NT),
                                         nums[:, 3, :].unsqueeze(1).to_broadcast([P, NT, E]), ALU.add))
            for r in range(2):
                step(nc.vector.tensor_tensor(picked, slot_all, hot[r], ALU.mult))
                step(nc.vector.tensor_reduce(slotf[:, r, :], picked, axis=AX_X, op=ALU.add))
            step(nc.vector.tensor_copy(slot[:], slotf))
            nc.vector.tensor_scalar(lo_i[:], slot[:], P - 1, None, ALU.bitwise_and)
            step(nc.vector.tensor_scalar(hi_i[:], slot[:], P.bit_length() - 1, None, ALU.logical_shift_right))
            nc.vector.tensor_copy(lo_f, lo_i[:].rearrange("p r t -> p (r t)"))
            step(nc.vector.tensor_copy(hi_f, hi_i[:].rearrange("p r t -> p (r t)")))
            step(nc.vector.tensor_tensor(hit_hi, js[:].unsqueeze(1).to_broadcast([P, R2, NE]),
                                         hi_f.unsqueeze(2).to_broadcast([P, R2, NE]), ALU.is_equal))
            assert steps[0] == TILES_MADE
            tile_rows(nc.vector, 0)
            step(one_hot_places(nc.vector, 0))
            assert steps[0] == ROWS_MADE
            for n in (1, 2):
                step(one_hot_places(nc.vector, n))
            dve.wait_ge(s_tok, 1)
            step(one_hot_places(nc.vector, 3))
            next_piece()
            step(nc.vector.tensor_tensor(before, nums[:, 2, :].unsqueeze(1).to_broadcast([P, NS, E]),
                                         js[:, 0:NS].unsqueeze(2).to_broadcast([P, NS, E]), ALU.is_le))
            step(nc.vector.tensor_reduce(expert_f, before, axis=AX_X, op=ALU.add))
            step(nc.vector.tensor_scalar(expert[:], expert_f, float(E - 1), None, ALU.min))
            step(nc.vector.tensor_tensor(start2, before[:, :, E - 1], js[:, 0:NS], ALU.mult))
            step(nc.vector.tensor_tensor(before, before, nums[:, 2, :].unsqueeze(1).to_broadcast([P, NS, E]), ALU.mult))
            step(nc.vector.tensor_reduce(start_f, before, axis=AX_X, op=ALU.max))
            step(nc.vector.tensor_tensor(start_i[:], start_f, start2, ALU.max))
            step(nc.vector.tensor_scalar(adds[:, 1, :], start_i[:], 1, None, ALU.logical_shift_right))
            step(nc.vector.tensor_tensor(adds[:, 0, :], start_i[:], adds[:, 1, :], ALU.subtract))
            step(nc.vector.tensor_scalar(adds[:], adds[:], 16.0, 16.0, ALU.mult, ALU.add))
            dve.wait_ge(s_tok, R2 // PT)
            step(nc.vector.tensor_copy(found, ps[2][:, 0:3 * NE].rearrange("p (a s) -> p a s", a=3)))
            nc.vector.tensor_copy(tok_w[:, 0, :], found[:, 0, 0:NS])
            step(nc.vector.tensor_tensor(tok_w[:, 1, :], found[:, 1, 0:NS], found[:, 2, 0:NS], ALU.add))
            step(nc.vector.tensor_scalar(spare_f, tok_w[:, 0, :], 0.0, spare[:], ALU.is_equal, ALU.mult))
            nc.vector.scalar_tensor_tensor(out=token[:], in0=tok_w[:, 0, :], scalar=-1.0, in1=spare_f,
                                           op0=ALU.add, op1=ALU.add).then_inc(s_route, 1)
            while later:
                next_piece()

            def slots_lo(j, k):
                dve.wait_ge(s_xghi, j + 1)
                nc.vector.tensor_tensor(xgT[:, k, LO], chunked(ps[k][:]), f32(xgT[:, k, HI]), ALU.subtract)\
                    .then_inc(s_xglo, 1)

            def hidden(j, k):
                dve.wait_ge(s_sg, j + 1)
                nc.vector.tensor_tensor(hid[:, k, 0:F], ps[2 + k][:, F:2 * F], sg[:, k, :], ALU.mult)
                nc.vector.tensor_tensor(hid[:, k, F:2 * P], ps[2 + k][:, F + P:2 * F], sg[:, k, P:F], ALU.mult)\
                    .then_inc(s_hid, 1)

            def hidden_lo(j, k):
                dve.wait_ge(s_hthi, j + 1)
                nc.vector.tensor_tensor(hidT[:, k, LO], ps[4 + k][:, 0:2 * P].rearrange("p (c n) -> p c n", c=2),
                                        f32(hidT[:, k, HI]), ALU.subtract).then_inc(s_htlo, 1)

            slots_lo(0, 0)
            slots_lo(1, 1)
            hidden(0, 0)
            slots_lo(2, 0)
            hidden(1, 1)
            hidden_lo(0, 0)
            slots_lo(3, 1)
            with dve.Fori(1, (NS - 3) // 2) as i:
                for k in range(2):
                    hidden(2 * i + k, k)
                    hidden_lo(2 * i + k - 1, 1 - k)
                    slots_lo(2 * i + k + 2, k)
            for j in range(NS - 3, NS + 1):
                if j < NS:
                    hidden(j, j % 2)
                hidden_lo(j - 1, (j - 1) % 2)
                if j + 2 < NS:
                    slots_lo(j + 2, j % 2)

        @block.tensor
        def _(pe):
            pe.wait_ge(s_const, 3)

            def free(key):
                order, banks, at = (tp_order, 2, tp_at) if key in tp_at else (pj_order, 3, pj_at)
                if at[key] >= banks:
                    kind, i = order[at[key] - banks]
                    pe.wait_ge(LAST[kind][0], LAST[kind][1](i))

            def stored(key):
                pe.wait_ge(LAST[key[0]][0], LAST[key[0]][1](key[1]))

            def transpose_tile(key, src, done):
                free(key)
                for c in range(C):
                    last = nc.tensor.transpose(bank(key)[:, c * P:(c + 1) * P], src[:, c * P:(c + 1) * P], ident[:])
                last.then_inc(done, 1)

            def product(out_ap, stationary, moving, first, last, check=True):
                passes = ((HI, HI), (HI, LO), (LO, HI))
                for n, (a, m) in enumerate(passes):
                    ins = nc.tensor.matmul(out_ap, stationary(a), moving(m), start=first and n == 0,
                                           stop=last and n == 2, skip_group_check=not check)
                return ins

            def project(key, stationary, moving, filled, chunk_ready=None):
                free(key)
                for c in range(C):
                    if chunk_ready is not None:
                        pe.wait_ge(s_wlo, chunk_ready + c)
                    last = product(bank(key)[:], lambda a: stationary(c, a), lambda a: moving(c, a), c == 0, c == C - 1)
                last.then_inc(filled, 1)

            def state(t):
                pe.wait_ge(s_kvlo, 2 * t + 2)
                if t == TB:
                    pe.wait_ge(s_stlo, G)
                i = t % TB
                for c in range(C):
                    cols = slice(c * P, (c + 1) * P)
                    last = product(kv_ps[:, cols], lambda a: k_sb[:, t % 2, a, cols], lambda a: v_sb[:, t % 2, a, cols],
                                   i == 0 and c == 0, i == TB - 1 and c == C - 1, check=False)
                last.then_inc(s_kvused, 1)

            def weight(w):
                return lambda c, a: w[:, a, c * D:(c + 1) * D]

            def x_transpose(t):
                pe.wait_ge(s_xn, t + 1)
                transpose_tile(("x", t), xn[:, t % 2, :], s_xf)

            def by_rows(t):
                at = t % TB * P
                return lambda c, a: xT[:, a, c, at:at + P]

            def q_block(g):
                at = g * BLK % TB * P
                for m in range(C):
                    project(("q", g * C + m), lambda c, a: wq[:, a, c * D + m * P:c * D + (m + 1) * P],
                            lambda c, a: xT[:, a, c, at:at + BLK * P], s_qf)

            def k_tile(t, chunk_ready=None):
                stored(("x", t))
                project(("k", t), by_rows(t), weight(wk), s_kvf, chunk_ready)

            def v_tile(t):
                project(("v", t), by_rows(t), weight(wv), s_kvf)

            x_transpose(0)
            x_transpose(1)
            for i in range(TB):
                k_tile(i, 1 if i == 0 else None)
                if i > 0:
                    state(i - 1)
                pe.wait_ge(s_wlo, C + 1)
                v_tile(i)
                if i + 2 < TB:
                    x_transpose(i + 2)
            pe.wait_ge(s_wlo, C + 4)
            pe.wait_ge(s_wr, 16)
            state(TB - 1)
            q_block(0)
            project(("u", 0), by_rows(0), weight(wu), s_uf)
            x_transpose(TB)
            for s in range(STEPS):
                if s < NT:
                    if s % BLK == 0:
                        stored(("q", s // BLK * C + C - 1))
                    if s % TB == 0:
                        pe.wait_ge(s_stlo, (s // TB + 1) * G)
                    if s >= 2:
                        pe.wait_ge(s_a1, s - 1)
                    o = s % BLK * P
                    for c in range(C):
                        last = product(o_ps[s % 2][:, c * P:(c + 1) * P], lambda a: qT[:, a, c, o:o + P],
                                       lambda a: kv_bd[:, a, c, :], True, True)
                    last.then_inc(s_of, 1)
                if 1 <= s < NT + 1:
                    pe.wait_ge(s_att, s)
                    transpose_tile(("a", s - 1), att[:, (s - 1) % 2, :], s_af)
                if s + 1 < NT:
                    project(("u", s + 1), by_rows(s + 1), weight(wu), s_uf)
                if s >= 2:
                    pe.wait_ge(s_h, s - 1)
                    transpose_tile(("h", s - 2), h_sb[:, s % 2, :], s_hf)
                if TB + s < NT:
                    k_tile(TB + s)
                    if s > 0:
                        state(TB + s - 1)
                    v_tile(TB + s)
                if s < NT - 1 and s % BLK == BLK - 1:
                    q_block(s // BLK + 1)
                if TB + s + 1 < NT:
                    x_transpose(TB + s + 1)
                if s == TB - 1:
                    state(NT - 1)
                if 1 <= s < NT + 1:
                    j = s - 1
                    stored(("a", j))
                    project(("p", j), lambda c, a: attT[:, j % 2, a, c, :], weight(wo), s_pf)
                if s >= 2:
                    j = s - 2
                    stored(("h", j))
                    free(("r", j))
                    for c in range(C):
                        last = nc.tensor.matmul(bank(("r", j))[:, 0:E], hT[:, j % 2, c, :], w_r[:, c, :],
                                                start=(c == 0), stop=(c == C - 1))
                    last.then_inc(s_rf, 1)

            pe.wait_ge(s_const, 15)
            pe.wait_ge(s_v, MASK_MADE)
            m2 = mask[:].rearrange("p t e -> p (t e)")
            pe.wait_ge(s_sc, NT)
            nc.tensor.matmul(ps[0][:, 0:NT * E], tri[:], m2, start=True, stop=True)
            for t in range(1, NT):
                nc.tensor.matmul(ps[0][:, t * E:NT * E], ones[:], m2[:, 0:(NT - t) * E], start=False,
                                 stop=True, skip_group_check=True)
            for t in range(NT):
                last = nc.tensor.matmul(ps[1][:, 0:E], ones[:], mask[:, t, :], start=(t == 0), stop=(t == NT - 1))
            last.then_inc(s_cnt, 1)
            for n in range(R2 // PT):
                pe.wait_ge(s_v, ROWS_MADE + n)
                if n == 2:
                    pe.wait_ge(s_second, 1)
                for r in range(n * PT, (n + 1) * PT):
                    last = nc.tensor.matmul(ps[2][:, 0:3 * NE], places[:, n % 3, r % PT, :],
                                            id_hi[:, r, :, :].rearrange("p a s -> p (a s)"),
                                            start=(r == 0), stop=(r == R2 - 1))
                last.then_inc(s_tok, 1)

            def transpose_slots(j, k, gathers):
                pe.wait_ge(s_xg[k], 16 * gathers)
                for c in range(C):
                    last = nc.tensor.transpose(ps[k][:, c * P:(c + 1) * P], xg[:, k, c * P:(c + 1) * P], ident[:])
                last.then_inc(s_xgt, 1)

            def of_expert(e, part, at, width):
                at += part * WE
                return w_ex[:, bass.ds(e, 1), at:at + width].rearrange("p a n -> p (a n)")

            def gate_up(j, k):
                e = pe.value_load(expert[0:1, bass.ds(j, 1)], min_val=0, max_val=E - 1)
                pe.wait_ge(s_xglo, j + 1)
                for c in range(C):
                    last = product(ps[2 + k][:, 0:2 * F], lambda a: xgT[:, k, a, c, :],
                                   lambda a: of_expert(e, a, c * 2 * F, 2 * F), c == 0, c == C - 1)
                last.then_inc(s_guf, 1)

            def transpose_hidden(j, k):
                pe.wait_ge(s_hid, j + 1)
                for c in range(2):
                    last = nc.tensor.transpose(ps[4 + k][:, c * P:(c + 1) * P], hid[:, k, c * P:(c + 1) * P], ident[:])
                last.then_inc(s_ht, 1)

            def down(j, k, stored):
                e = pe.value_load(expert[0:1, bass.ds(j, 1)], min_val=0, max_val=E - 1)
                pe.wait_ge(s_htlo, j + 1)
                if stored is not None:
                    pe.wait_ge(s_ys, stored)
                product(ps[6 + k][:], lambda a: hidT[:, k, a, 0, :],
                        lambda a: of_expert(e, a, GU, D), True, False)
                nc.tensor.matmul(ps[6 + k][:], hidT[:, k, HI, 1, :], of_expert(e, HI, WL, D), start=False, stop=False)
                nc.tensor.matmul(ps[6 + k][:], hidT[:, k, LO, 1, :], of_expert(e, HI, WL, D), start=False, stop=True)\
                    .then_inc(s_yf, 1)

            pe.wait_ge(s_route, 1)
            transpose_slots(0, 0, 1)
            transpose_slots(1, 1, 1)
            pe.wait_ge(s_elo, lo_count(False))
            pe.wait_ge(s_elop, lo_count(True))
            for j in range(4):
                gate_up(j, j % 2)
                if j >= 1:
                    transpose_hidden(j - 1, 1 - j % 2)
                transpose_slots(j + 2, j % 2, (j + 2) // 2 + 1)
                if j >= 2:
                    down(j - 2, j % 2, None)
            with pe.Fori(2, (NS - 3) // 2) as i:
                for k in range(2):
                    gate_up(2 * i + k, k)
                    transpose_hidden(2 * i + k - 1, 1 - k)
                    transpose_slots(2 * i + k + 2, k, i + 2)
                    down(2 * i + k - 2, k, 2 * i + k - 3)
            for j in range(NS - 3, NS + 2):
                if j < NS:
                    gate_up(j, j % 2)
                if j - 1 < NS:
                    transpose_hidden(j - 1, (j - 1) % 2)
                if j + 2 < NS:
                    transpose_slots(j + 2, j % 2, (j + 2) // 2 + 1)
                down(j - 2, j % 2, j - 3)


def kernel(**inputs):
    import numpy as np
    import concourse.bacc as bacc
    from concourse.bass_utils import run_bass_kernel_spmd

    def at(name):
        return np.asarray(inputs["L0_" + name])

    def chunks(w):
        return w.T.reshape(C, P, w.shape[0]).transpose(1, 0, 2).reshape(P, C * w.shape[0])

    x = at("attn_x")
    T = x.shape[0] * x.shape[1]
    gate, up, down = at("ffn_w_gate_proj"), at("ffn_w_up_proj"), at("ffn_w_down_proj")
    experts = []
    for e in range(E):
        d = down[e].T
        experts.append(np.concatenate([chunks(np.concatenate([gate[e], up[e]])), d[0:P],
                                       np.concatenate([d[P:F], d[P:F]])], axis=1))
    arrays = {
        "x": x.reshape(T, D),
        "wqkvuo": np.stack([chunks(at("attn_" + n)) for n in ("wq", "wk", "wv", "wu", "wo")]),
        "wrouter": chunks(at("ffn_w_gate_router")).reshape(P, C, E),
        "wexperts": np.stack(experts),
    }
    arrays = {k: np.ascontiguousarray(v) for k, v in arrays.items()}
    nc = bacc.Bacc("TRN2", target_bir_lowering=False, num_devices=1)
    args = {k: nc.dram_tensor("in_" + k, v.shape, mybir.dt.from_np(v.dtype), kind="ExternalInput").ap()
            for k, v in arrays.items()}
    h_dram = nc.dram_tensor("h_rows", (T + P, D), F32, kind="Internal").ap()
    out = nc.dram_tensor("out", (T + P, D), F32, kind="ExternalOutput").ap()
    attention_and_moe(nc, h_dram=h_dram, out=out, **args)
    r = run_bass_kernel_spmd(nc, [{"in_" + k: v for k, v in arrays.items()}], core_ids=[0])
    return r.results[0]["out"][0:T].reshape(x.shape)
```

```python
from contextlib import ExitStack

import concourse.bass as bass
from concourse import mybir

ALU = mybir.AluOpType
ACT = mybir.ActivationFunctionType
F32 = mybir.dt.float32
F32R = mybir.dt.float32r
BF16 = mybir.dt.bfloat16
I32 = mybir.dt.int32
U32 = mybir.dt.uint32
AX_X = mybir.AxisListType.X

P = 128
D = 512
C = D // P
HD = 32
H = D // HD
G = P // HD
E = 8
F = 192
FB = F - P
GU = C * 2 * F
WE = GU + 2 * D
WL = GU + D
PIECES = 4
PIECE = WE // PIECES
EPS = 1e-5


def attention_and_moe(nc, x, wqkvuo, wrouter, wexperts, h_dram, out):
    T = x.shape[0]
    B = 2
    L = T // B
    NT = T // P
    TB = L // P
    BLK = 4
    NS = (2 * T + E * (P - 1)) // P
    NE = NS + NS % 2
    R2 = 2 * NT
    PT = NT // 2
    NW = 5
    XB = 3
    EB = 6
    STEPS = NT + 2
    EARLY = 20
    HI, LO = 0, 1


    with ExitStack() as ctx:
        def sb(name, shape, dt=F32):
            return ctx.enter_context(nc.sbuf_tensor(name, shape, dt))

        def sem(name):
            return ctx.enter_context(nc.semaphore(name))

        class Arena:

            def __init__(self, name, size, dt):
                self.t, self.size, self.at = sb(name, [P, size], dt), size, 0

            def take(self, *shape):
                n = 1
                for d in shape:
                    n *= d
                a, self.at = self.at, self.at + n
                assert self.at <= self.size, (self.at, self.size)
                v = self.t[:, a:self.at]
                names = "abcde"[:len(shape)]
                if len(shape) > 1:
                    v = v.rearrange(f"p ({' '.join(names)}) -> p {' '.join(names)}",
                                    **{m: d for m, d in zip(names[1:], shape[1:])})
                return v

        parts = Arena("parts", NW * 2 * C * D + 2 * C * L + 2 * C * BLK * P + 2 * 2 * 2 * D + 2 * C * P + 2 * 2 * C * P,
                      F32R)
        wk, wv = parts.take(2, C * D), parts.take(2, C * D)
        k_sb = parts.take(2, 2, D)
        v_sb = parts.take(2, 2, D)
        wq = parts.take(2, C * D)
        xT = parts.take(2, C, L)
        wu = parts.take(2, C * D)
        qT = parts.take(2, C, BLK * P)
        kv_bd = parts.take(2, C, P)
        wo = parts.take(2, C * D)
        attT = parts.take(2, 2, C, P)
        parts.at = 0
        w_ex = parts.take(E, WE + WL)
        xgT = parts.take(2, 2, C, P)
        hidT = parts.take(2, 2, 2, P)
        LATE = (E - 1) * PIECES
        parts.at = (E - 1) * (WE + WL)
        places = parts.take(3, PT, P)
        pair_rows = parts.take(R2, 3, NE)
        prob_hi = parts.take(2, NT)

        rows = Arena("rows", EB * PIECE + 15 * D, F32)
        x_in = rows.take(XB, D)
        xn = rows.take(2, D)
        rows.at = 0
        e_raw = rows.take(EB, PIECE)
        slots_at = rows.at
        x_res = rows.take(2, D)
        x1 = rows.take(2, D)
        sq = rows.take(2, D)
        stage_at = rows.at
        att = rows.take(2, D)
        u = rows.take(2, D)
        h_sb = rows.take(2, D)
        hT = rows.take(2, C, P)
        zero = rows.take(D)
        rows.at = stage_at
        w_raw = rows.take(2, C * D)
        rows.at = slots_at
        xg = rows.take(2, D)
        sg = rows.take(2, F)
        hid = rows.take(2, 2 * P)
        y_sb = rows.take(2, D)
        rows.at = slots_at
        hot = rows.take(2, NT, E)
        slot_all = rows.take(NT, E)
        picked = rows.take(2, NT, E)
        above = rows.take(E, NT)
        hit_hi = rows.take(R2, NE)
        rows.at = slots_at + 2 * (D + F + 2 * P + D)
        before = rows.take(NS, E)
        top_idf, slotf = rows.take(2, NT), rows.take(2, NT)
        prob, prob_lo = rows.take(2, NT), rows.take(2, NT)
        found = rows.take(2, NE)
        spare_f, expert_f, start_f = [rows.take(NS) for _ in range(3)]
        lo_f, hi_f = rows.take(R2), rows.take(R2)

        w_r = sb("w_r", [P, C, E])
        ident = sb("ident", [P, P])
        expo = sb("expo", [P, H])
        bstat = sb("bstat", [P, 6])
        mv = sb("mv", [P, 4, 2])
        rstd = sb("rstd", [P, 4])
        ss = sb("ss", [P, 2, H])
        rn = sb("rn", [P, 2, H])
        rn_in = sb("rn_in", [P, H])
        scores = sb("scores", [P, NT, E])
        top = sb("top", [P, NT, E])
        top_id = sb("top_id", [P, NT, E], U32)
        mask = sb("mask", [P, NT, E], BF16)
        iota_e = sb("iota_e", [P, E])
        iota_lo = sb("iota_lo", [P, P])
        thresh = sb("thresh", [P, NT])
        below = sb("below", [P, E, E])
        js = sb("js", [P, NE])
        nums = sb("nums", [P, 3, E])
        slot = sb("slot", [P, 2, NT], I32)
        lo_i = sb("lo_i", [P, 2, NT], I32)
        hi_i = sb("hi_i", [P, 2, NT], I32)
        id1 = sb("id1", [P, NT])
        spare = sb("spare", [P, NE])
        tri = sb("tri", [P, P], BF16)
        ones = sb("ones", [P, P], BF16)
        slot_w = sb("slot_w", [P, NS])
        token = sb("token", [P, NS], U32)
        expert = sb("expert", [P, NS], I32)
        start_i = sb("start_i", [P, NS], I32)
        adds = sb("adds", [P, 2, NS], I32)
        pick = sb("pick", [P, 2], U32)
        put = sb("put", [P, 2], U32)
        state_sum = sb("state_sum", [P, C, HD])
        gap = sb("gap", [P, NT])
        egap = sb("egap", [P, NT])

        ps = [ctx.enter_context(nc.psum_tensor(f"ps{i}", [P, 512], F32)) for i in range(8)]
        tp = ps[0:2]
        pj = ps[2:5]
        kv_ps = [ps[1], ps[5]]
        o_ps = ps[6:8]

        s_wk = [sem(f"wk_loaded{c}") for c in range(C)]
        s_w = {n: sem(f"w{n}_loaded") for n in "qvuo"}
        s_wr = sem("router_loaded")
        s_x = [sem(f"x_loaded{i}") for i in range(XB)]
        s_xr = [sem(f"x_reloaded{i}") for i in range(2)]
        s_er = [sem(f"experts_loaded{i}") for i in range(EB)]
        s_x1sv = [sem(f"x1_saved{i}") for i in range(2)]
        s_hsv = [sem(f"h_saved{i}") for i in range(2)]
        s_const = sem("constants_made")
        s_whi, s_wlo = sem("weight_hi_made"), sem("weight_lo_made")
        s_ehi, s_elo, s_elop = sem("expert_hi_made"), sem("expert_lo_made"), sem("expert_lo_made_by_pool")
        s_bst, s_var = sem("stats_made"), sem("var_made")
        s_rsi, s_rstd = sem("rstd_base_made"), sem("rstd_made")
        s_xn, s_h = sem("xn_made"), sem("h_made")
        s_xf, s_xhi, s_xlo = sem("x_transposed"), sem("xT_hi_stored"), sem("xT_lo_stored")
        s_kvf, s_kvhi, s_kvlo = sem("k_or_v_filled"), sem("k_or_v_hi_stored"), sem("k_or_v_lo_stored")
        s_kvused, s_st, s_stlo = sem("kv_used"), sem("state_step"), sem("state_lo_stored")
        s_qf, s_qhi, s_qlo = sem("q_filled"), sem("q_hi_stored"), sem("q_lo_stored")
        s_uf, s_us = sem("u_filled"), sem("u_stored")
        s_of, s_sq, s_ss = sem("o_filled"), sem("squares_made"), sem("square_sums_made")
        s_rni, s_rn = sem("norm_base_made"), sem("norm_made")
        s_a1, s_att = sem("gated"), sem("normed")
        s_af, s_ahi, s_alo = sem("att_transposed"), sem("attT_hi_stored"), sem("attT_lo_stored")
        s_pf, s_x1 = sem("attn_out_filled"), sem("x1_made")
        s_hf, s_hst = sem("h_transposed"), sem("hT_stored")
        s_rf, s_sc = sem("scores_filled"), sem("scores_stored")
        s_top, s_topid = sem("top_scores_made"), sem("top_ids_made")
        GAP_MADE, MASK_MADE, TILES_MADE, ROWS_MADE = 1, 4, 21, 22
        s_v = sem("routing_step")
        s_second = sem("second_rows_made")
        s_table = sem("tables_made")
        s_cnt, s_eg, s_tok, s_route = sem("ranks_filled"), sem("exp_made"), sem("tokens_filled"), sem("routing_made")
        s_pick, s_put = sem("pick_made"), sem("put_made")
        s_xg = [sem(f"gathered{i}") for i in range(2)]
        s_xgt, s_xghi, s_xglo = sem("slots_transposed"), sem("slots_hi_stored"), sem("slots_lo_stored")
        s_guf, s_sg, s_hid = sem("gateup_filled"), sem("silu_made"), sem("hidden_made")
        s_ht, s_hthi, s_htlo = sem("hidden_transposed"), sem("hidden_hi_stored"), sem("hidden_lo_stored")
        s_yf, s_ys = sem("y_filled"), sem("y_stored")
        s_zero = sem("spare_rows_zero")
        s_add = [sem(f"added{i}") for i in range(2)]

        tp_order = [("x", 0), ("x", 1)] + [("x", i + 2) for i in range(TB - 2)] + [("x", TB)]
        pj_order = [(name, i) for i in range(TB) for name in "kv"] + [("q", m) for m in range(C)] + [("u", 0)]
        ln_order = [("x", i) for i in range(TB + 2)]
        for s in range(STEPS):
            if 1 <= s < NT + 1:
                tp_order.append(("a", s - 1))
            if s + 1 < NT:
                pj_order.append(("u", s + 1))
            if s >= 2:
                tp_order.append(("h", s - 2))
            if TB + s < NT:
                pj_order += [("k", TB + s), ("v", TB + s)]
            if s < NT - 1 and s % BLK == BLK - 1:
                pj_order += [("q", (s // BLK + 1) * C + m) for m in range(C)]
            if TB + s + 1 < NT:
                tp_order.append(("x", TB + s + 1))
            if TB + s + 2 < NT:
                ln_order.append(("x", TB + s + 2))
            if 1 <= s < NT + 1:
                pj_order.append(("p", s - 1))
                ln_order.append(("y", s - 1))
            if s >= 2:
                pj_order.append(("r", s - 2))
        tp_at = {key: n for n, key in enumerate(tp_order)}
        one_bank = tp_at["a", TB]
        pj_at = {key: n for n, key in enumerate(pj_order)}
        ln_at = {key: n for n, key in enumerate(ln_order)}
        LAST = {"x": (s_xlo, lambda i: i + 1), "a": (s_alo, lambda i: i + 1), "h": (s_hst, lambda i: i + 1),
                "k": (s_kvlo, lambda i: 2 * i + 1), "v": (s_kvlo, lambda i: 2 * i + 2),
                "u": (s_us, lambda i: i + 1), "q": (s_qlo, lambda i: i + 1),
                "p": (s_x1, lambda i: i + 1), "r": (s_sc, lambda i: i + 1)}

        def step_of(n):
            return TB + n // 2 if n < 3 * PIECES else STEPS - 3 + (n - 3 * PIECES + 1) // 3

        def by_pool(n):
            return n >= EARLY and n % PIECES != PIECES - 1 and n != LATE + 1

        def lo_count(pool):
            return sum(by_pool(n) == pool for n in range(E * PIECES))

        def lo_made(n):
            return (s_elop if by_pool(n) else s_elo), sum(by_pool(m) == by_pool(n) for m in range(n + 1))

        def place_free(n):
            e = n // PIECES
            if e < 2:
                return s_kvused, NT
            if e < 3:
                return s_qf, NT // BLK * C
            if e < 6:
                return s_uf, NT
            if n >= LATE:
                return s_tok, R2 // PT
            return s_pf, NT

        def tile_rows(engine, first, count):
            pairs = slice(first, first + count)
            r, tiles = first // NT, slice(first % NT, first % NT + count)
            for a, factor in enumerate((id1[:, tiles], prob_hi[:, r, tiles].bitcast(F32), prob_lo[:, r, tiles])):
                last = engine.tensor_tensor(pair_rows[:, pairs, a, :], hit_hi[:, pairs, :],
                                            factor.unsqueeze(2).to_broadcast([P, count, NE]), ALU.mult)
            return last

        def one_hot_places(engine, n):
            return engine.tensor_tensor(places[:, n % 3], iota_lo[:].unsqueeze(1).to_broadcast([P, PT, P]),
                                        lo_f[:, n * PT:(n + 1) * PT].unsqueeze(2).to_broadcast([P, PT, P]),
                                        ALU.is_equal)

        def split_lo(eng, engine, n):
            e, c = n // PIECES, n % PIECES * PIECE
            width = max(0, min(PIECE, WL - c))
            eng.wait_ge(s_ehi, n + 1)
            ins = engine.tensor_tensor(w_ex[:, e, WE + c:WE + c + width], e_raw[:, n % EB, 0:width],
                                       w_ex[:, e, c:c + width].bitcast(F32), ALU.subtract)
            if width < PIECE:
                ins = engine.tensor_tensor(w_ex[FB:P, e, WL:WE], e_raw[FB:P, n % EB, width:PIECE],
                                           w_ex[FB:P, e, WL:WE].bitcast(F32), ALU.subtract)
            ins.then_inc(s_elop if by_pool(n) else s_elo, 1)

        def ln_buffer(key):
            return key[1] % 2 + (2 if key[0] == "y" else 0)

        def bank(key):
            return tp[max(0, tp_at[key] - one_bank) % 2] if key in tp_at else pj[pj_at[key] % 3]

        def chunked(ap):
            return ap.rearrange("p (c n) -> p c n", c=C)

        block = ctx.enter_context(nc.Block())

        @block.sync
        def _(sp):
            def load_x(t):
                if t >= XB:
                    sp.wait_ge(s_xn, t - XB + 1)
                sp.dma_start(x_in[:, t % XB, :], x[t * P:(t + 1) * P, :]).then_inc(s_x[t % XB], 16)

            def reload_x(t):
                if t >= 2:
                    sp.wait_ge(s_x1, t - 1)
                sp.dma_start(x_res[:, t % 2, :], x[t * P:(t + 1) * P, :]).then_inc(s_xr[t % 2], 16)

            def load_weight(name, at, k, split):
                if split:
                    sp.wait_ge(s_wlo, split)
                sp.dma_start(w_raw[:, k, :], wqkvuo[at]).then_inc(s_w[name], 16)

            def load_piece(n):
                if n >= EB:
                    sp.wait_ge(*lo_made(n - EB))
                else:
                    sp.wait_ge(s_xf, NT)
                c = n % PIECES * PIECE
                sp.dma_start(e_raw[:, n % EB, :], wexperts[n // PIECES, :, c:c + PIECE]).then_inc(s_er[n % EB], 16)

            load_x(0)
            load_x(1)
            for c in range(C):
                sp.dma_start(w_raw[:, 0, c * D:(c + 1) * D], wqkvuo[1, :, c * D:(c + 1) * D]).then_inc(s_wk[c], 16)
            load_weight("v", 2, 1, 0)
            for t in range(2, 5):
                load_x(t)
            for i in range(TB):
                if i == 0:
                    load_weight("q", 0, 0, C)
                if i == 1:
                    load_weight("u", 3, 1, C + 1)
                if i == 2:
                    load_weight("o", 4, 0, C + 2)
                    sp.dma_start(w_r[:], wrouter).then_inc(s_wr, 16)
                if i + 5 < TB + XB:
                    load_x(i + 5)
            reload_x(0)
            reload_x(1)
            load_x(TB + XB)
            for s in range(STEPS):
                if s >= 2:
                    sp.wait_ge(s_h, s - 1)
                    sp.dma_start(h_dram[(s - 2) * P:(s - 1) * P, :], h_sb[:, s % 2, :]).then_inc(s_hsv[s % 2], 16)
                if TB + XB + 1 + s < NT:
                    load_x(TB + XB + 1 + s)
                for n in range(E * PIECES):
                    if n < EARLY and step_of(n) == s + 1:
                        load_piece(n)
                if 1 <= s < NT + 1:
                    j = s - 1
                    sp.wait_ge(s_x1, s)
                    sp.dma_start(out[j * P:s * P, :], x1[:, j % 2, :]).then_inc(s_x1sv[j % 2], 16)
                    if s + 1 < NT:
                        reload_x(s + 1)
            for n in range(EARLY, E * PIECES):
                load_piece(n)
            for k in range(2):
                sp.wait_ge(s_add[k], 16 * (1 + (NS + 1 - k) // 2))

        @block.gpsimd
        def _(pool):
            def made(ins):
                ins.then_inc(s_const, 1)

            def iota(ap, pattern, base=0, channel=0):
                made(nc.gpsimd.iota(ap, pattern=pattern, base=base, channel_multiplier=channel,
                                    allow_small_or_imprecise_dtypes=True))

            made(nc.gpsimd.memset(ident[:], 0.0))
            made(nc.gpsimd.memset(expo[:], -0.5))
            pool.wait_ge(s_const, 2)
            made(nc.gpsimd.affine_select(out=ident[:], in_=ident[:], compare_op=ALU.not_equal, fill=1.0,
                                         base=0, pattern=[[-1, P]], channel_multiplier=1))
            made(nc.gpsimd.memset(tri[:], 0.0))
            made(nc.gpsimd.memset(ones[:], 1.0))
            made(nc.gpsimd.memset(below[:], float(P)))
            made(nc.gpsimd.memset(zero, 0.0))
            pool.wait_ge(s_const, 7)
            made(nc.gpsimd.affine_select(out=tri[:], in_=tri[:], compare_op=ALU.is_ge, fill=1.0,
                                         base=0, pattern=[[-1, P]], channel_multiplier=1))
            made(nc.gpsimd.affine_select(out=below[:], in_=below[:], compare_op=ALU.is_ge, fill=0.0,
                                         base=-1, pattern=[[1, E], [-1, E]], channel_multiplier=0))
            iota(id1[:], [[P, NT]], base=1, channel=1)
            iota(spare[:], [[0, NE // 2], [P, 2]], base=T + 1, channel=1)
            iota(iota_e[:], [[1, E]])
            iota(iota_lo[:], [[1, P]])
            iota(thresh[:], [[P, NT]])
            iota(js[:], [[1, NE]])

            def inverse_deviation(n, k):
                pool.wait_ge(s_rsi, n)
                nc.gpsimd.tensor_tensor(rstd[:, k:k + 1], rstd[:, k:k + 1], expo[:, 0:1], ALU.pow).then_inc(s_rstd, 1)

            def inverse_norms(t):
                pool.wait_ge(s_ss, t + 1)
                nc.gpsimd.tensor_scalar(rn_in[:], ss[:, t % 2, :], 1e-24, float(HD * HD), ALU.max, ALU.mult)\
                    .then_inc(s_rni, 1)
                pool.wait_ge(s_rni, t + 1)
                nc.gpsimd.tensor_tensor(rn[:, t % 2, :], rn_in[:], expo[:], ALU.pow).then_inc(s_rn, 1)

            for i in range(TB + 2):
                inverse_deviation(i + 1, ln_buffer(("x", i)))
            for k in range(2):
                rows_k = slice(T + k * P, T + (k + 1) * P)
                nc.gpsimd.dma_start(h_dram[rows_k, :], zero).then_inc(s_zero, 16)
                nc.gpsimd.dma_start(out[rows_k, :], zero).then_inc(s_add[k], 16)
            for s in range(STEPS):
                if s < NT:
                    inverse_norms(s)
                if TB + s + 2 < NT:
                    inverse_deviation(ln_at["x", TB + s + 2] + 1, ln_buffer(("x", TB + s + 2)))
                if 1 <= s < NT + 1:
                    inverse_deviation(ln_at["y", s - 1] + 1, ln_buffer(("y", s - 1)))

            for n in range(EARLY, LATE):
                if n == LATE - PIECES + 1:
                    pool.wait_ge(s_v, TILES_MADE)
                    for first in (NT, NT + PT):
                        tile_rows(nc.gpsimd, first, PT).then_inc(s_second, 1)
                if by_pool(n):
                    split_lo(pool, nc.gpsimd, n)

            def gather(j, k, gathered, transposed):
                if gathered is not None:
                    pool.wait_ge(s_xg[k], 16 * gathered)
                if transposed is not None:
                    pool.wait_ge(s_xgt, transposed)
                nc.gpsimd.tensor_copy(pick[:, k:k + 1], token[:, bass.ds(j, 1)]).then_inc(s_pick, 1)
                pool.wait_ge(s_pick, j + 1)
                pool.nop(nofuse=True)
                nc.gpsimd.indirect_dma_start(
                    out=xg[:, k, :], out_offset=None, in_=h_dram,
                    in_offset=bass.IndirectOffsetOnAxis(ap=pick[:, k:k + 1], axis=0)).then_inc(s_xg[k], 16)

            def add(j, k, before):
                if before is not None:
                    pool.wait_ge(s_add[k], 16 * before)
                need = [pool.value_load(adds[0:1, r, bass.ds(j, 1)], min_val=16, max_val=16 * (NS + 1))
                        for r in range(2)]
                nc.gpsimd.tensor_copy(put[:, k:k + 1], token[:, bass.ds(j, 1)]).then_inc(s_put, 1)
                for r in range(2):
                    pool.wait_ge(s_add[r], need[r])
                pool.wait_ge(s_ys, j + 1)
                pool.wait_ge(s_put, j + 1)
                pool.nop(nofuse=True)
                nc.gpsimd.indirect_dma_start(
                    out=out, out_offset=bass.IndirectOffsetOnAxis(ap=put[:, k:k + 1], axis=0),
                    in_=y_sb[:, k, :], in_offset=None, compute_op=ALU.add).then_inc(s_add[k], 16)

            pool.wait_ge(s_route, 1)
            for k in range(2):
                pool.wait_ge(s_hsv[k], 16 * (NT // 2))
                pool.wait_ge(s_x1sv[k], 16 * (NT // 2))
                pool.wait_ge(s_add[k], 16)
            pool.wait_ge(s_zero, 32)
            gather(0, 0, None, None)
            gather(1, 1, None, None)
            for n in range(LATE, E * PIECES):
                if by_pool(n):
                    split_lo(pool, nc.gpsimd, n)
            for j in range(2, 6):
                gather(j, j % 2, j // 2, j - 1)
            pool.wait_ge(s_table, 1)
            with pool.Fori(1, (NS - 5) // 2) as i:
                for k in range(2):
                    gather(2 * i + k + 4, k, i + 2, 2 * i + k + 3)
                    add(2 * i + k - 2, k, i)
            gather(NS - 1, 0, (NS - 1) // 2, NS - 2)
            for j in range(NS - 7, NS):
                add(j, j % 2, j // 2 + 1)

        @block.scalar
        def _(act):
            def weight_hi(name, dst, k):
                act.wait_ge(s_w[name], 16)
                nc.scalar.activation(dst[:, HI, :], w_raw[:, k, :], ACT.Copy).then_inc(s_whi, 1)

            def hi(filled, count, dst, key, func, done, shaped=True):
                act.wait_ge(filled, count)
                src = bank(key)[:]
                nc.scalar.activation(dst, chunked(src) if shaped else src, func).then_inc(done, 1)

            def x_hi(t):
                at = t % TB * P
                hi(s_xf, t + 1, xT[:, HI, :, at:at + P], ("x", t), ACT.Copy, s_xhi)

            def k_hi(t):
                if t >= 2:
                    act.wait_ge(s_kvused, t - 1)
                hi(s_kvf, 2 * t + 1, k_sb[:, t % 2, HI, :], ("k", t), ACT.Relu, s_kvhi, False)

            def v_hi(t):
                hi(s_kvf, 2 * t + 2, v_sb[:, t % 2, HI, :], ("v", t), ACT.Copy, s_kvhi, False)

            def q_hi(g):
                for m in range(C):
                    hi(s_qf, g * C + m + 1, qT[:, HI, m, :], ("q", g * C + m), ACT.Relu, s_qhi, False)

            def u_silu(t):
                if t >= 2:
                    act.wait_ge(s_att, t - 1)
                hi(s_uf, t + 1, u[:, t % 2, :], ("u", t), ACT.Silu, s_us, False)

            def expert_hi(n):
                e, c = n // PIECES, n % PIECES * PIECE
                act.wait_ge(s_er[n % EB], 16 * (n // EB + 1))
                act.wait_ge(*place_free(n))
                nc.scalar.activation(w_ex[:, e, c:c + PIECE], e_raw[:, n % EB, :], ACT.Copy).then_inc(s_ehi, 1)

            for c in range(C):
                if c == C - 1:
                    x_hi(0)
                act.wait_ge(s_wk[c], 16)
                nc.scalar.activation(wk[:, HI, c * D:(c + 1) * D], w_raw[:, 0, c * D:(c + 1) * D], ACT.Copy)\
                    .then_inc(s_whi, 1)
            weight_hi("v", wv, 1)
            x_hi(1)
            for i in range(TB):
                k_hi(i)
                v_hi(i)
                if i + 2 < TB:
                    x_hi(i + 2)
                if i == 1:
                    weight_hi("q", wq, 0)
                if i == 2:
                    weight_hi("u", wu, 1)
                if i == 3:
                    weight_hi("o", wo, 0)
            q_hi(0)
            u_silu(0)
            x_hi(TB)
            def squares(t):
                act.wait_ge(s_of, t + 1)
                if t >= 2:
                    act.wait_ge(s_ss, t - 1)
                nc.scalar.activation(sq[:, t % 2, :], o_ps[t % 2][:], ACT.Square,
                                     scale=1.0 / (HD * HD ** 0.5)).then_inc(s_sq, 1)

            for s in range(STEPS):
                if s < NT:
                    squares(s)
                if 1 <= s < NT + 1:
                    j = s - 1
                    if j >= 2:
                        act.wait_ge(s_pf, j - 1)
                    hi(s_af, j + 1, attT[:, j % 2, HI], ("a", j), ACT.Copy, s_ahi)
                for n in range(EARLY):
                    if step_of(n) == s:
                        expert_hi(n)
                if s + 1 < NT:
                    u_silu(s + 1)
                if s >= 2:
                    j = s - 2
                    if j >= 2:
                        act.wait_ge(s_rf, j - 1)
                    hi(s_hf, j + 1, hT[:, j % 2], ("h", j), ACT.Copy, s_hst)
                if TB + s < NT:
                    k_hi(TB + s)
                    v_hi(TB + s)
                if s < NT - 1 and s % BLK == BLK - 1:
                    q_hi(s // BLK + 1)
                if TB + s + 1 < NT:
                    x_hi(TB + s + 1)

            act.wait_ge(s_v, GAP_MADE)
            nc.scalar.activation(egap[:], gap[:], ACT.Exp).then_inc(s_eg, 1)
            for n in range(EARLY, E * PIECES):
                expert_hi(n)

            def slots_hi(j, k):
                act.wait_ge(s_xgt, j + 1)
                nc.scalar.activation(xgT[:, k, HI], chunked(ps[k][:]), ACT.Copy).then_inc(s_xghi, 1)

            def silu(j, k):
                act.wait_ge(s_guf, j + 1)
                nc.scalar.activation(sg[:, k, :], ps[2 + k][:, 0:F], ACT.Silu).then_inc(s_sg, 1)

            def hidden_hi(j, k):
                act.wait_ge(s_ht, j + 1)
                nc.scalar.activation(hidT[:, k, HI], ps[4 + k][:, 0:2 * P].rearrange("p (c n) -> p c n", c=2),
                                     ACT.Copy).then_inc(s_hthi, 1)

            def store_y(j, k, added):
                act.wait_ge(s_yf, j + 1)
                if added is not None:
                    act.wait_ge(s_add[k], 16 * added)
                nc.scalar.activation(y_sb[:, k, :], ps[6 + k][:], ACT.Copy, scale=slot_w[:, bass.ds(j, 1)])\
                    .then_inc(s_ys, 1)

            act.wait_ge(s_route, 1)
            slots_hi(0, 0)
            slots_hi(1, 1)
            silu(0, 0)
            slots_hi(2, 0)
            silu(1, 1)
            hidden_hi(0, 0)
            slots_hi(3, 1)
            act.wait_ge(s_table, 1)
            with act.Fori(1, (NS - 3) // 2) as i:
                for k in range(2):
                    silu(2 * i + k, k)
                    hidden_hi(2 * i + k - 1, 1 - k)
                    slots_hi(2 * i + k + 2, k)
                    store_y(2 * i + k - 2, k, i)
            for j in range(NS - 3, NS + 2):
                if j < NS:
                    silu(j, j % 2)
                if j - 1 < NS:
                    hidden_hi(j - 1, (j - 1) % 2)
                if j + 2 < NS:
                    slots_hi(j + 2, j % 2)
                store_y(j - 2, j % 2, (j - 2) // 2 + 1)

        @block.vector
        def _(dve):
            f32 = lambda ap: ap.bitcast(F32)

            nc.vector.memset(f32(kv_bd), 0.0).then_inc(s_st, 1)

            def weight_lo(n, w, k):
                dve.wait_ge(s_whi, C + n + 1)
                nc.vector.tensor_tensor(w[:, LO, :], w_raw[:, k, :], f32(w[:, HI, :]), ALU.subtract).then_inc(s_wlo, 1)

            def statistics(row, key):
                n, k = ln_at[key], ln_buffer(key)
                nc.vector.bn_stats(bstat[:], row).then_inc(s_bst, 1)
                dve.wait_ge(s_bst, n + 1)
                nc.vector.bn_aggr(mv[:, k, :], bstat[:]).then_inc(s_var, 1)
                dve.wait_ge(s_var, n + 1)
                nc.vector.tensor_scalar(rstd[:, k:k + 1], mv[:, k, 1:2], EPS, None, ALU.add).then_inc(s_rsi, 1)

            def normalised(dst, row, key, done):
                k = ln_buffer(key)
                dve.wait_ge(s_rstd, ln_at[key] + 1)
                nc.vector.tensor_scalar(dst, row, mv[:, k, 0:1], rstd[:, k:k + 1], ALU.subtract, ALU.mult)\
                    .then_inc(done, 1)

            def lo(his, count, dst, key, high, op, done, shaped=True):
                dve.wait_ge(his, count)
                src = chunked(bank(key)[:]) if shaped else bank(key)[:]
                if op is None:
                    nc.vector.tensor_tensor(dst, src, f32(high), ALU.subtract).then_inc(done, 1)
                else:
                    nc.vector.scalar_tensor_tensor(out=dst, in0=src, scalar=0.0, in1=f32(high), op0=op,
                                                   op1=ALU.subtract).then_inc(done, 1)

            def x_stats(t):
                dve.wait_ge(s_x[t % XB], 16 * (t // XB + 1))
                statistics(x_in[:, t % XB, :], ("x", t))

            def x_norm(t):
                if t >= 2:
                    dve.wait_ge(s_xf, t - 1)
                normalised(xn[:, t % 2, :], x_in[:, t % XB, :], ("x", t), s_xn)

            def x_lo(t):
                at = t % TB * P
                lo(s_xhi, t + 1, xT[:, LO, :, at:at + P], ("x", t), xT[:, HI, :, at:at + P], None, s_xlo)

            def k_lo(t):
                lo(s_kvhi, 2 * t + 1, k_sb[:, t % 2, LO, :], ("k", t), k_sb[:, t % 2, HI, :], ALU.max, s_kvlo, False)

            def v_lo(t):
                lo(s_kvhi, 2 * t + 2, v_sb[:, t % 2, LO, :], ("v", t), v_sb[:, t % 2, HI, :], None, s_kvlo, False)

            def store_state(b):
                dve.wait_ge(s_kvused, (b + 1) * TB)
                if b:
                    dve.wait_ge(s_of, b * TB)
                for q in range(G):
                    rng = slice(q * HD, (q + 1) * HD)
                    for n in range(2):
                        src = kv_ps[n][rng, :].rearrange("p (c a d) -> p c d a", c=2, a=2)[:, :, rng, :]
                        nc.vector.tensor_reduce(state_sum[rng, 2 * n:2 * n + 2, :], src, axis=AX_X, op=ALU.add)\
                            .then_inc(s_st, 1)
                dve.wait_ge(s_st, b * 3 * G + 2 * G + 1)
                for q in range(G):
                    rng = slice(q * HD, (q + 1) * HD)
                    nc.vector.tensor_copy(kv_bd[rng, HI, :, rng], state_sum[rng]).then_inc(s_st, 1)
                dve.wait_ge(s_st, (b + 1) * 3 * G + 1)
                for q in range(G):
                    rng = slice(q * HD, (q + 1) * HD)
                    nc.vector.tensor_tensor(kv_bd[rng, LO, :, rng], state_sum[rng], f32(kv_bd[rng, HI, :, rng]),
                                            ALU.subtract).then_inc(s_stlo, 1)

            def q_lo(g):
                for m in range(C):
                    lo(s_qhi, g * C + m + 1, qT[:, LO, m, :], ("q", g * C + m), qT[:, HI, m, :], ALU.max, s_qlo, False)
                    if m == 0 and g * BLK % TB == 0:
                        store_state(g * BLK // TB)

            def square_sums(t):
                dve.wait_ge(s_sq, t + 1)
                nc.vector.tensor_reduce(ss[:, t % 2, :], sq[:, t % 2, :].rearrange("p (h e) -> p h e", e=HD),
                                        axis=AX_X, op=ALU.add).then_inc(s_ss, 1)

            def h_rows(t):
                if t >= 2:
                    dve.wait_ge(s_hf, t - 1)
                    dve.wait_ge(s_hsv[t % 2], 16 * (t // 2))
                normalised(h_sb[:, t % 2, :], x1[:, t % 2, :], ("y", t), s_h)

            def store_scores(t):
                dve.wait_ge(s_rf, t + 1)
                nc.vector.tensor_copy(scores[:, t, :], bank(("r", t))[:, 0:E]).then_inc(s_sc, 1)

            def top_scores(t):
                dve.wait_ge(s_sc, t + 1)
                nc.vector.max(top[:, t, :], scores[:, t, :]).then_inc(s_top, 1)

            def top_ids(t):
                dve.wait_ge(s_top, t + 1)
                nc.vector.max_index(top_id[:, t, :], top[:, t, :], scores[:, t, :]).then_inc(s_topid, 1)

            def wk_lo(c):
                part = slice(c * D, (c + 1) * D)
                dve.wait_ge(s_whi, c + 1)
                nc.vector.tensor_tensor(wk[:, LO, part], w_raw[:, 0, part], f32(wk[:, HI, part]), ALU.subtract)\
                    .then_inc(s_wlo, 1)

            x_stats(0)
            x_stats(1)
            x_norm(0)
            wk_lo(0)
            x_norm(1)
            wk_lo(1)
            x_lo(0)
            wk_lo(2)
            wk_lo(3)
            weight_lo(0, wv, 1)
            x_lo(1)
            x_stats(2)
            for i in range(TB):
                k_lo(i)
                if i + 2 < TB:
                    x_norm(i + 2)
                if i + 3 < TB + 1:
                    x_stats(i + 3)
                v_lo(i)
                if i + 2 < TB:
                    x_lo(i + 2)
                if i == 1:
                    weight_lo(1, wq, 0)
                if i == 2:
                    weight_lo(2, wu, 1)
                if i == 3:
                    weight_lo(3, wo, 0)
            x_norm(TB)
            x_stats(TB + 1)
            q_lo(0)
            x_lo(TB)
            for s in range(STEPS):
                if s < NT:
                    square_sums(s)
                if s >= 3:
                    store_scores(s - 3)
                if 2 <= s < NT - 1:
                    h_rows(s - 2)
                if 1 <= s < NT + 1:
                    j = s - 1
                    lo(s_ahi, j + 1, attT[:, j % 2, LO], ("a", j), attT[:, j % 2, HI], None, s_alo)
                if s >= NT - 1:
                    h_rows(s - 2)
                if s >= 4:
                    top_scores(s - 4)
                if s >= 5:
                    top_ids(s - 5)
                for n in range(EARLY):
                    if step_of(n) == s:
                        split_lo(dve, nc.vector, n)
                if s < NT:
                    heads = att[:, s % 2, :].rearrange("p (h e) -> p h e", e=HD)
                    dve.wait_ge(s_us, s + 1)
                    if s >= 2:
                        dve.wait_ge(s_af, s - 1)
                    nc.vector.tensor_tensor(att[:, s % 2, :], o_ps[s % 2][:], u[:, s % 2, :], ALU.mult)\
                        .then_inc(s_a1, 1)
                    dve.wait_ge(s_a1, s + 1)
                    dve.wait_ge(s_rn, s + 1)
                    nc.vector.tensor_tensor(heads, heads, rn[:, s % 2, :].unsqueeze(2).to_broadcast([P, H, HD]),
                                            ALU.mult).then_inc(s_att, 1)
                if TB + s < NT:
                    k_lo(TB + s)
                    if TB + s + 1 < NT:
                        x_norm(TB + s + 1)
                    if TB + s + 2 < NT:
                        x_stats(TB + s + 2)
                    v_lo(TB + s)
                if s < NT - 1 and s % BLK == BLK - 1:
                    q_lo(s // BLK + 1)
                if TB + s + 1 < NT:
                    x_lo(TB + s + 1)
                if 1 <= s < NT + 1:
                    j = s - 1
                    dve.wait_ge(s_pf, j + 1)
                    dve.wait_ge(s_xr[j % 2], 16 * (j // 2 + 1))
                    if j >= 2:
                        dve.wait_ge(s_x1sv[j % 2], 16 * (j // 2))
                    nc.vector.tensor_tensor(x1[:, j % 2, :], bank(("p", j))[:], x_res[:, j % 2, :], ALU.add)\
                        .then_inc(s_x1, 1)
                    dve.wait_ge(s_x1, j + 1)
                    statistics(x1[:, j % 2, :], ("y", j))
            store_scores(NT - 1)
            top_scores(NT - 2)
            top_scores(NT - 1)
            for t in range(NT - 3, NT):
                top_ids(t)
            for k in range(2):
                dve.wait_ge(s_x1sv[k], 16 * (NT // 2))
                dve.wait_ge(s_hsv[k], 16 * (NT // 2))

            steps = [0]

            def step(ins):
                steps[0] += 1
                ins.then_inc(s_v, 1)
                dve.wait_ge(s_v, steps[0])

            later = [n for n in range(EARLY, E * PIECES) if not by_pool(n)]

            def next_piece():
                split_lo(dve, nc.vector, later.pop(0))

            dve.wait_ge(s_const, 15)
            dve.wait_ge(s_top, NT)
            step(nc.vector.tensor_tensor(gap[:], top[:, :, 1], top[:, :, 0], ALU.subtract))
            assert steps[0] == GAP_MADE
            dve.wait_ge(s_topid, NT)
            step(nc.vector.tensor_copy(top_idf, top_id[:, :, 0:2].rearrange("p t r -> p r t")))
            dve.wait_ge(s_add[0], 16)
            dve.wait_ge(s_add[1], 16)
            dve.wait_ge(s_zero, 32)
            for r in range(2):
                last = nc.vector.tensor_tensor(hot[:, r], iota_e[:].unsqueeze(1).to_broadcast([P, NT, E]),
                                               top_idf[:, r, :].unsqueeze(2).to_broadcast([P, NT, E]), ALU.is_equal)
            step(last)
            step(nc.vector.tensor_tensor(mask[:], hot[:, 0], hot[:, 1], ALU.add))
            assert steps[0] == MASK_MADE
            dve.wait_ge(s_eg, 1)
            step(nc.vector.tensor_scalar(gap[:], egap[:], 1.0, None, ALU.add))
            step(nc.vector.reciprocal(prob[:, 0, :], gap[:]))
            step(nc.vector.tensor_tensor(prob[:, 1, :], prob[:, 0, :], egap[:], ALU.mult))
            step(nc.vector.tensor_copy(prob_hi, prob))
            step(nc.vector.tensor_tensor(prob_lo, prob, f32(prob_hi), ALU.subtract))
            dve.wait_ge(s_cnt, 1)
            step(nc.vector.tensor_tensor(above, ps[1][:, 0:E].unsqueeze(2).to_broadcast([P, E, NT]),
                                         thresh[:].unsqueeze(1).to_broadcast([P, E, NT]), ALU.is_gt))
            step(nc.vector.tensor_reduce(nums[:, 0, :], above, axis=AX_X, op=ALU.add))
            step(nc.vector.tensor_tensor(before[:, 0:E, :], nums[:, 0, :].unsqueeze(1).to_broadcast([P, E, E]),
                                         below[:], ALU.mult))
            step(nc.vector.tensor_reduce(nums[:, 2, :], before[:, 0:E, :], axis=AX_X, op=ALU.add))
            step(nc.vector.tensor_tensor(slot_all, ps[0][:, 0:NT * E].rearrange("p (t e) -> p t e", t=NT),
                                         nums[:, 2, :].unsqueeze(1).to_broadcast([P, NT, E]), ALU.add))
            for r in range(2):
                last = nc.vector.tensor_tensor(picked[:, r], slot_all, hot[:, r], ALU.mult)
            step(last)
            step(nc.vector.tensor_reduce(slotf, picked, axis=AX_X, op=ALU.add))
            step(nc.vector.tensor_copy(slot[:], slotf))
            nc.vector.tensor_scalar(lo_i[:], slot[:], P - 1, None, ALU.bitwise_and)
            step(nc.vector.tensor_scalar(hi_i[:], slot[:], P.bit_length() - 1, None, ALU.logical_shift_right))
            nc.vector.tensor_copy(lo_f, lo_i[:].rearrange("p r t -> p (r t)"))
            step(nc.vector.tensor_copy(hi_f, hi_i[:].rearrange("p r t -> p (r t)")))
            def tile_hits(first, end):
                step(nc.vector.tensor_tensor(
                    hit_hi[:, first:end, :], js[:].unsqueeze(1).to_broadcast([P, end - first, NE]),
                    hi_f[:, first:end].unsqueeze(2).to_broadcast([P, end - first, NE]), ALU.is_equal))

            tile_hits(0, PT)
            tile_rows(nc.vector, 0, PT)
            tile_hits(PT, R2)
            assert steps[0] == TILES_MADE
            step(one_hot_places(nc.vector, 0))
            assert steps[0] == ROWS_MADE
            tile_rows(nc.vector, PT, PT)
            for n in (1, 2):
                step(one_hot_places(nc.vector, n))
            dve.wait_ge(s_tok, 1)
            step(one_hot_places(nc.vector, 3))
            step(nc.vector.scalar_tensor_tensor(out=nums[:, 1, :], in0=nums[:, 2, :], scalar=1.0 / P,
                                                in1=nums[:, 0, :], op0=ALU.mult, op1=ALU.add))
            step(nc.vector.tensor_tensor(before, nums[:, 1, :].unsqueeze(1).to_broadcast([P, NS, E]),
                                         js[:, 0:NS].unsqueeze(2).to_broadcast([P, NS, E]), ALU.is_le))
            step(nc.vector.tensor_reduce(expert_f, before, axis=AX_X, op=ALU.add))
            next_piece()
            dve.wait_ge(s_tok, R2 // PT)
            step(nc.vector.scalar_tensor_tensor(out=spare_f, in0=ps[2][:, 0:NS], scalar=0.0, in1=spare[:, 0:NS],
                                                op0=ALU.is_equal, op1=ALU.mult))
            nc.vector.scalar_tensor_tensor(out=token[:], in0=ps[2][:, 0:NS], scalar=-1.0, in1=spare_f,
                                           op0=ALU.add, op1=ALU.add).then_inc(s_route, 1)
            step(nc.vector.tensor_copy(found, ps[2][:, NE:3 * NE].rearrange("p (a s) -> p a s", a=2)))
            step(nc.vector.tensor_tensor(slot_w[:], found[:, 0, 0:NS], found[:, 1, 0:NS], ALU.add))
            step(nc.vector.tensor_scalar(expert[:], expert_f, float(E - 1), None, ALU.min))
            step(nc.vector.tensor_tensor(before, before, nums[:, 1, :].unsqueeze(1).to_broadcast([P, NS, E]), ALU.mult))
            step(nc.vector.tensor_reduce(start_f, before, axis=AX_X, op=ALU.max))
            step(nc.vector.tensor_copy(start_i[:], start_f))
            step(nc.vector.tensor_scalar(adds[:, 1, :], start_i[:], 1, None, ALU.logical_shift_right))
            step(nc.vector.tensor_tensor(adds[:, 0, :], start_i[:], adds[:, 1, :], ALU.subtract))
            nc.vector.tensor_scalar(adds[:], adds[:], 16.0, 16.0, ALU.mult, ALU.add).then_inc(s_table, 1)
            while later:
                next_piece()

            def slots_lo(j, k):
                dve.wait_ge(s_xghi, j + 1)
                nc.vector.tensor_tensor(xgT[:, k, LO], chunked(ps[k][:]), f32(xgT[:, k, HI]), ALU.subtract)\
                    .then_inc(s_xglo, 1)

            def hidden(j, k):
                dve.wait_ge(s_sg, j + 1)
                nc.vector.tensor_tensor(hid[:, k, 0:F], ps[2 + k][:, F:2 * F], sg[:, k, :], ALU.mult)
                nc.vector.tensor_tensor(hid[:, k, F:2 * P], ps[2 + k][:, F + P:2 * F], sg[:, k, P:F], ALU.mult)\
                    .then_inc(s_hid, 1)

            def hidden_lo(j, k):
                dve.wait_ge(s_hthi, j + 1)
                nc.vector.tensor_tensor(hidT[:, k, LO], ps[4 + k][:, 0:2 * P].rearrange("p (c n) -> p c n", c=2),
                                        f32(hidT[:, k, HI]), ALU.subtract).then_inc(s_htlo, 1)

            slots_lo(0, 0)
            slots_lo(1, 1)
            hidden(0, 0)
            slots_lo(2, 0)
            hidden(1, 1)
            hidden_lo(0, 0)
            slots_lo(3, 1)
            with dve.Fori(1, (NS - 3) // 2) as i:
                for k in range(2):
                    hidden(2 * i + k, k)
                    hidden_lo(2 * i + k - 1, 1 - k)
                    slots_lo(2 * i + k + 2, k)
            for j in range(NS - 3, NS + 1):
                if j < NS:
                    hidden(j, j % 2)
                hidden_lo(j - 1, (j - 1) % 2)
                if j + 2 < NS:
                    slots_lo(j + 2, j % 2)

        @block.tensor
        def _(pe):
            pe.wait_ge(s_const, 3)

            def free(key):
                order, at = (tp_order, tp_at) if key in tp_at else (pj_order, pj_at)
                banks = 3 if key in pj_at else 1 if at[key] <= one_bank + 1 else 2
                if at[key] >= banks:
                    kind, i = order[at[key] - banks]
                    pe.wait_ge(LAST[kind][0], LAST[kind][1](i))

            def stored(key):
                pe.wait_ge(LAST[key[0]][0], LAST[key[0]][1](key[1]))

            def transpose_tile(key, src, done):
                free(key)
                for c in range(C):
                    last = nc.tensor.transpose(bank(key)[:, c * P:(c + 1) * P], src[:, c * P:(c + 1) * P], ident[:])
                last.then_inc(done, 1)

            def product(out_ap, stationary, moving, first, last, check=True):
                passes = ((HI, HI), (HI, LO), (LO, HI))
                for n, (a, m) in enumerate(passes):
                    ins = nc.tensor.matmul(out_ap, stationary(a), moving(m), start=first and n == 0,
                                           stop=last and n == 2, skip_group_check=not check)
                return ins

            def project(key, stationary, moving, filled, chunk_ready=None):
                free(key)
                for c in range(C):
                    if chunk_ready is not None:
                        pe.wait_ge(s_wlo, chunk_ready + c)
                    last = product(bank(key)[:], lambda a: stationary(c, a), lambda a: moving(c, a), c == 0, c == C - 1)
                last.then_inc(filled, 1)

            def state(t):
                pe.wait_ge(s_kvlo, 2 * t + 2)
                if t == TB:
                    pe.wait_ge(s_stlo, G)
                first, end = t % TB == 0, t % TB == TB - 1
                for c in range(C):
                    cols = slice(c * P, (c + 1) * P)
                    at = c % 2 * 2 * P
                    nc.tensor.matmul(kv_ps[c // 2][:, at:at + 2 * P].rearrange("p (a n) -> p a n", a=2),
                                     k_sb[:, t % 2, HI, cols], v_sb[:, t % 2, :, cols],
                                     start=first and c % 2 == 0, stop=end and c % 2 == 1, skip_group_check=True)
                    last = nc.tensor.matmul(kv_ps[c // 2][:, at:at + P], k_sb[:, t % 2, LO, cols],
                                            v_sb[:, t % 2, HI, cols], start=False, stop=end and c % 2 == 1,
                                            skip_group_check=True)
                last.then_inc(s_kvused, 1)

            def weight(w):
                return lambda c, a: w[:, a, c * D:(c + 1) * D]

            def x_transpose(t):
                pe.wait_ge(s_xn, t + 1)
                transpose_tile(("x", t), xn[:, t % 2, :], s_xf)

            def by_rows(t):
                at = t % TB * P
                return lambda c, a: xT[:, a, c, at:at + P]

            def q_block(g):
                at = g * BLK % TB * P
                for m in range(C):
                    project(("q", g * C + m), lambda c, a: wq[:, a, c * D + m * P:c * D + (m + 1) * P],
                            lambda c, a: xT[:, a, c, at:at + BLK * P], s_qf)
                    if m == 0 and g * BLK % TB == 0:
                        state((g * BLK // TB + 1) * TB - 1)

            def k_tile(t, chunk_ready=None):
                stored(("x", t))
                project(("k", t), by_rows(t), weight(wk), s_kvf, chunk_ready)

            def v_tile(t):
                project(("v", t), by_rows(t), weight(wv), s_kvf)

            def h_transpose(t):
                pe.wait_ge(s_h, t + 1)
                transpose_tile(("h", t), h_sb[:, t % 2, :], s_hf)

            def o_tile(t):
                if t % BLK == 0:
                    stored(("q", t // BLK * C + C - 1))
                if t % TB == 0:
                    pe.wait_ge(s_stlo, (t // TB + 1) * G)
                if t >= 2:
                    pe.wait_ge(s_a1, t - 1)
                o = t % BLK * P
                for c in range(C):
                    last = product(o_ps[t % 2][:, c * P:(c + 1) * P], lambda a: qT[:, a, c, o:o + P],
                                   lambda a: kv_bd[:, a, c, :], True, True)
                last.then_inc(s_of, 1)

            x_transpose(0)
            x_transpose(1)
            for i in range(TB):
                k_tile(i, 1 if i == 0 else None)
                if i > 0:
                    state(i - 1)
                pe.wait_ge(s_wlo, C + 1)
                v_tile(i)
                if i + 2 < TB:
                    x_transpose(i + 2)
            pe.wait_ge(s_wlo, C + 4)
            pe.wait_ge(s_wr, 16)
            q_block(0)
            project(("u", 0), by_rows(0), weight(wu), s_uf)
            x_transpose(TB)
            for s in range(STEPS):
                if s < NT:
                    o_tile(s)
                if 1 <= s < NT + 1:
                    pe.wait_ge(s_att, s)
                    transpose_tile(("a", s - 1), att[:, (s - 1) % 2, :], s_af)
                if s + 1 < NT:
                    project(("u", s + 1), by_rows(s + 1), weight(wu), s_uf)
                if 2 <= s < NT - 1:
                    h_transpose(s - 2)
                if TB + s < NT:
                    k_tile(TB + s)
                    if s > 0:
                        state(TB + s - 1)
                    v_tile(TB + s)
                if s < NT - 1 and s % BLK == BLK - 1:
                    q_block(s // BLK + 1)
                if TB + s + 1 < NT:
                    x_transpose(TB + s + 1)
                if 1 <= s < NT + 1:
                    j = s - 1
                    stored(("a", j))
                    project(("p", j), lambda c, a: attT[:, j % 2, a, c, :], weight(wo), s_pf)
                if s >= NT - 1:
                    h_transpose(s - 2)
                if s >= 2:
                    j = s - 2
                    stored(("h", j))
                    free(("r", j))
                    for c in range(C):
                        last = nc.tensor.matmul(bank(("r", j))[:, 0:E], hT[:, j % 2, c, :], w_r[:, c, :],
                                                start=(c == 0), stop=(c == C - 1))
                    last.then_inc(s_rf, 1)

            pe.wait_ge(s_const, 15)
            pe.wait_ge(s_v, MASK_MADE)
            m2 = mask[:].rearrange("p t e -> p (t e)")
            pe.wait_ge(s_sc, NT)
            nc.tensor.matmul(ps[0][:, 0:NT * E], tri[:], m2, start=True, stop=True)
            for t in range(1, NT):
                nc.tensor.matmul(ps[0][:, t * E:NT * E], ones[:], m2[:, 0:(NT - t) * E], start=False,
                                 stop=True, skip_group_check=True)
            for t in range(NT):
                last = nc.tensor.matmul(ps[1][:, 0:E], ones[:], mask[:, t, :], start=(t == 0), stop=(t == NT - 1))
            last.then_inc(s_cnt, 1)
            for n in range(R2 // PT):
                pe.wait_ge(s_v, ROWS_MADE + n)
                if n >= 2:
                    pe.wait_ge(s_second, n - 1)
                for r in range(n * PT, (n + 1) * PT):
                    last = nc.tensor.matmul(ps[2][:, 0:3 * NE], places[:, n % 3, r % PT, :],
                                            pair_rows[:, r, :, :].rearrange("p a s -> p (a s)"),
                                            start=(r == 0), stop=(r == R2 - 1))
                last.then_inc(s_tok, 1)

            def transpose_slots(j, k, gathers):
                pe.wait_ge(s_xg[k], 16 * gathers)
                for c in range(C):
                    last = nc.tensor.transpose(ps[k][:, c * P:(c + 1) * P], xg[:, k, c * P:(c + 1) * P], ident[:])
                last.then_inc(s_xgt, 1)

            def of_expert(e, part, at, width):
                at += part * WE
                return w_ex[:, bass.ds(e, 1), at:at + width].rearrange("p a n -> p (a n)")

            def gate_up(j, k):
                e = pe.value_load(expert[0:1, bass.ds(j, 1)], min_val=0, max_val=E - 1)
                pe.wait_ge(s_xglo, j + 1)
                for c in range(C):
                    last = product(ps[2 + k][:, 0:2 * F], lambda a: xgT[:, k, a, c, :],
                                   lambda a: of_expert(e, a, c * 2 * F, 2 * F), c == 0, c == C - 1)
                last.then_inc(s_guf, 1)

            def transpose_hidden(j, k):
                pe.wait_ge(s_hid, j + 1)
                for c in range(2):
                    last = nc.tensor.transpose(ps[4 + k][:, c * P:(c + 1) * P], hid[:, k, c * P:(c + 1) * P], ident[:])
                last.then_inc(s_ht, 1)

            def down(j, k, stored):
                e = pe.value_load(expert[0:1, bass.ds(j, 1)], min_val=0, max_val=E - 1)
                pe.wait_ge(s_htlo, j + 1)
                if stored is not None:
                    pe.wait_ge(s_ys, stored)
                product(ps[6 + k][:], lambda a: hidT[:, k, a, 0, :],
                        lambda a: of_expert(e, a, GU, D), True, False)
                nc.tensor.matmul(ps[6 + k][:], hidT[:, k, HI, 1, :], of_expert(e, HI, WL, D), start=False, stop=False)
                nc.tensor.matmul(ps[6 + k][:], hidT[:, k, LO, 1, :], of_expert(e, HI, WL, D), start=False, stop=True)\
                    .then_inc(s_yf, 1)

            pe.wait_ge(s_route, 1)
            transpose_slots(0, 0, 1)
            transpose_slots(1, 1, 1)
            pe.wait_ge(s_table, 1)
            pe.wait_ge(s_elo, lo_count(False))
            pe.wait_ge(s_elop, lo_count(True))
            for j in range(4):
                gate_up(j, j % 2)
                if j >= 1:
                    transpose_hidden(j - 1, 1 - j % 2)
                transpose_slots(j + 2, j % 2, (j + 2) // 2 + 1)
                if j >= 2:
                    down(j - 2, j % 2, None)
            with pe.Fori(2, (NS - 3) // 2) as i:
                for k in range(2):
                    gate_up(2 * i + k, k)
                    transpose_hidden(2 * i + k - 1, 1 - k)
                    transpose_slots(2 * i + k + 2, k, i + 2)
                    down(2 * i + k - 2, k, 2 * i + k - 3)
            for j in range(NS - 3, NS + 2):
                if j < NS:
                    gate_up(j, j % 2)
                if j - 1 < NS:
                    transpose_hidden(j - 1, (j - 1) % 2)
                if j + 2 < NS:
                    transpose_slots(j + 2, j % 2, (j + 2) // 2 + 1)
                down(j - 2, j % 2, j - 3)


def kernel(**inputs):
    import numpy as np
    import concourse.bacc as bacc
    from concourse.bass_utils import run_bass_kernel_spmd

    def at(name):
        return np.asarray(inputs["L0_" + name])

    def chunks(w):
        return w.T.reshape(C, P, w.shape[0]).transpose(1, 0, 2).reshape(P, C * w.shape[0])

    x = at("attn_x")
    T = x.shape[0] * x.shape[1]
    gate, up, down = at("ffn_w_gate_proj"), at("ffn_w_up_proj"), at("ffn_w_down_proj")
    experts = []
    for e in range(E):
        d = down[e].T
        experts.append(np.concatenate([chunks(np.concatenate([gate[e], up[e]])), d[0:P],
                                       np.concatenate([d[P:F], d[P:F]])], axis=1))
    arrays = {
        "x": x.reshape(T, D),
        "wqkvuo": np.stack([chunks(at("attn_" + n)) for n in ("wq", "wk", "wv", "wu", "wo")]),
        "wrouter": chunks(at("ffn_w_gate_router")).reshape(P, C, E),
        "wexperts": np.stack(experts),
    }
    arrays = {k: np.ascontiguousarray(v) for k, v in arrays.items()}
    nc = bacc.Bacc("TRN2", target_bir_lowering=False, num_devices=1)
    args = {k: nc.dram_tensor("in_" + k, v.shape, mybir.dt.from_np(v.dtype), kind="ExternalInput").ap()
            for k, v in arrays.items()}
    h_dram = nc.dram_tensor("h_rows", (T + 2 * P, D), F32, kind="Internal").ap()
    out = nc.dram_tensor("out", (T + 2 * P, D), F32, kind="ExternalOutput").ap()
    attention_and_moe(nc, h_dram=h_dram, out=out, **args)
    r = run_bass_kernel_spmd(nc, [{"in_" + k: v for k, v in arrays.items()}], core_ids=[0])
    return r.results[0]["out"][0:T].reshape(x.shape)
```
